# Optimizing a Trainium2 kernel written in Bass

```python
import numpy as np
import jax
import jax.numpy as jnp

def _softmax(x, axis=-1):
    return jax.nn.softmax(x, axis=axis)
def _gelu(x):
    return jax.nn.gelu(x, approximate=True)
def _silu(x):
    return jax.nn.silu(x)
def _sigmoid(x):
    return jax.nn.sigmoid(x)
def _layernorm(x, axis=-1, eps=1e-5):
    m = jnp.mean(x, axis=axis, keepdims=True)
    v = jnp.var(x, axis=axis, keepdims=True)
    return (x - m) / jnp.sqrt(v + eps)
def _scatter_add(tgt, idx, src, axis=0):
    return tgt.at[idx].add(src)
def _segment_sum(src, seg, n):
    return jax.ops.segment_sum(src, seg, n)

kernel_name = 'mk_conv_preact_d4_conv_nhwc192_991a51'

def setup_inputs(seed: int = 0):
    np.random.seed(seed)
    _w = jnp.asarray
    def _rec_inputs():
        import jax
        import jax.numpy as jnp
        _gk = jax.random.key(seed)
        x = -0.0001538 + 1 * jax.random.normal(jax.random.fold_in(_gk, 1), (8, 64, 64, 192), jnp.float32)
        return x
    x = _rec_inputs()
    def _L0_conv_setup():
        import jax, jax.numpy as jnp
        import numpy as np
        DIM = 192
        NH = 6
        EXP = 2
        DSTATE = 64
        NG = 1
        CHUNK = 256
        DCONV = 4
        DIN = DIM * EXP
        HD = DIN // NH
        CONVDIM = DIN + 2 * NG * DSTATE
        DPROJ = 2 * DIN + 2 * NG * DSTATE + NH
        B_, H_, W_ = (8, 64, 64)

        def layernorm(x, w, b, eps=1e-05):
            mu = jnp.mean(x, -1, keepdims=True)
            v = jnp.mean(jnp.square(x - mu), -1, keepdims=True)
            return (x - mu) * jax.lax.rsqrt(v + eps) * w + b

        def dwconv2d(x_nchw, w, b):
            y = jax.lax.conv_general_dilated(x_nchw, w, (1, 1), 'SAME', feature_group_count=x_nchw.shape[1], dimension_numbers=('NCHW', 'OIHW', 'NCHW'))
            return y + b[None, :, None, None]

        def causal_conv1d(x, w, b):
            K = w.shape[1]
            L = x.shape[1]
            xp = jnp.pad(x, ((0, 0), (K - 1, 0), (0, 0)))
            y = sum((xp[:, k:k + L, :] * w[:, k] for k in range(K)))
            return y + b

        def ssd(x, dt, A, Bm, Cm, chunk):
            b, l, h, p = x.shape
            n = Bm.shape[-1]
            nc = l // chunk
            x = x.reshape(b, nc, chunk, h, p)
            dt = dt.reshape(b, nc, chunk, h)
            Bm = Bm.reshape(b, nc, chunk, n)
            Cm = Cm.reshape(b, nc, chunk, n)
            dA = dt * A
            dA_cs = jnp.cumsum(dA, axis=2)
            seg = dA_cs[:, :, :, None, :] - dA_cs[:, :, None, :, :]
            mask = jnp.tril(jnp.ones((chunk, chunk), bool))
            seg = jnp.where(mask[None, None, :, :, None], seg, -1e+30)
            scores = jnp.einsum('bcin,bcjn->bcij', Cm, Bm)[..., None] * jnp.exp(seg) * dt[:, :, None, :, :]
            y = jnp.einsum('bcijh,bcjhp->bcihp', scores, x)
            decay_last = jnp.exp(dA_cs[:, :, -1:, :] - dA_cs)
            states = jnp.einsum('bcjn,bcjh,bcjhp->bchnp', Bm, dt * decay_last, x)
            chunk_decay = jnp.exp(dA_cs[:, :, -1, :])

            def step(carry, inp):
                s, cd = inp
                new = carry * cd[:, :, None, None] + s
                return (new, carry)
            init = jnp.zeros((b, h, n, p), x.dtype)
            _, prev = jax.lax.scan(step, init, (states.swapaxes(0, 1), chunk_decay.swapaxes(0, 1)))
            prev = prev.swapaxes(0, 1)
            y = y + jnp.einsum('bcin,bchnp,bcih->bcihp', Cm, prev, jnp.exp(dA_cs))
            return y.reshape(b, l, h, p)
        key = jax.random.key(seed)
        ks = jax.random.split(key, 12)
        n = lambda k, s, sc=0.02: jax.random.normal(k, s, jnp.float32) * sc
        return dict(x=jax.random.normal(ks[0], (B_, H_, W_, DIM), jnp.float32), cpe1_w=n(ks[1], (DIM, 1, 3, 3), 0.1), cpe1_b=jnp.zeros((DIM,), jnp.float32), ln1_w=jnp.ones((DIM,), jnp.float32), ln1_b=jnp.zeros((DIM,), jnp.float32), in_proj_w=n(ks[2], (DPROJ, DIM)), conv1d_w=n(ks[3], (CONVDIM, DCONV), 0.1), conv1d_b=jnp.zeros((CONVDIM,), jnp.float32), dt_bias=n(ks[4], (NH,), 0.1), A_log=jnp.log(jax.random.uniform(ks[5], (NH,), jnp.float32, 1.0, 16.0)), D_skip=jnp.ones((NH,), jnp.float32), rms_w=jnp.ones((DIN,), jnp.float32), out_proj_w=n(ks[6], (DIM, DIN)), cpe2_w=n(ks[7], (DIM, 1, 3, 3), 0.1), cpe2_b=jnp.zeros((DIM,), jnp.float32), ln2_w=jnp.ones((DIM,), jnp.float32), ln2_b=jnp.zeros((DIM,), jnp.float32), fc1_w=n(ks[8], (DIM * 4, DIM)), fc1_b=jnp.zeros((DIM * 4,), jnp.float32), fc2_w=n(ks[9], (DIM, DIM * 4)), fc2_b=jnp.zeros((DIM,), jnp.float32))
    _L0_conv_all = _L0_conv_setup()
    _L0_conv_in = {k: v for k, v in _L0_conv_all.items() if k in ('cpe1_w', 'cpe1_b', 'ln1_w', 'ln1_b', 'in_proj_w', 'conv1d_w', 'conv1d_b', 'dt_bias', 'A_log', 'D_skip', 'rms_w', 'out_proj_w', 'cpe2_w', 'cpe2_b', 'ln2_w', 'ln2_b', 'fc1_w', 'fc1_b', 'fc2_w', 'fc2_b', )}
    del _L0_conv_all

    def _L1_conv_setup():
        import jax, jax.numpy as jnp
        import numpy as np
        B, H, W, C = (4, 64, 64, 192)
        EXPAND, DSTATE, DCONV = (2, 16, 3)
        DIN = EXPAND * C
        DTR = -(-C // 16)
        K = 4

        def _ss2d(x, in_proj_w, conv_w, conv_b, x_proj_weight, dt_projs_weight, dt_projs_bias, A_logs, Ds, out_norm_w, out_norm_b, out_proj_w):
            Bn, Hh, Ww, Cm = x.shape
            L = Hh * Ww
            Din = conv_w.shape[0]
            N = A_logs.shape[-1]
            R = dt_projs_weight.shape[-1]
            xz = jnp.einsum('bhwc,oc->bhwo', x, in_proj_w)
            xa, z = jnp.split(xz, 2, axis=-1)
            xc = jnp.transpose(xa, (0, 3, 1, 2))
            xc = jax.lax.conv_general_dilated(xc, conv_w, (1, 1), 'SAME', feature_group_count=Din, dimension_numbers=('NCHW', 'OIHW', 'NCHW')) + conv_b[None, :, None, None]
            xc = jax.nn.silu(xc)
            x_flat = xc.reshape(Bn, Din, L)
            x_trans = jnp.transpose(xc, (0, 1, 3, 2)).reshape(Bn, Din, L)
            x_hwwh = jnp.stack([x_flat, x_trans], axis=1)
            xs = jnp.concatenate([x_hwwh, jnp.flip(x_hwwh, axis=-1)], axis=1)
            x_dbl = jnp.einsum('bkdl,kcd->bkcl', xs, x_proj_weight)
            dts, Bs, Cs = jnp.split(x_dbl, [R, R + N], axis=2)
            dts = jnp.einsum('bkrl,kdr->bkdl', dts, dt_projs_weight)
            A = -jnp.exp(A_logs).reshape(4, Din, N)
            delta = jax.nn.softplus(dts + dt_projs_bias[None, :, :, None])

            def step(h, inp):
                u_l, d_l, B_l, C_l = inp
                dA = jnp.exp(d_l[..., None] * A)
                dBu = d_l[..., None] * B_l[:, :, None, :] * u_l[..., None]
                h = dA * h + dBu
                y = jnp.sum(h * C_l[:, :, None, :], axis=-1)
                return (h, y)
            inputs = (jnp.moveaxis(xs, -1, 0), jnp.moveaxis(delta, -1, 0), jnp.moveaxis(Bs, -1, 0), jnp.moveaxis(Cs, -1, 0))
            h0 = jnp.zeros((Bn, 4, Din, N), xs.dtype)
            _, ys = jax.lax.scan(step, h0, inputs)
            out_y = jnp.moveaxis(ys, 0, -1) + xs * Ds.reshape(4, Din)[None, :, :, None]
            inv_y = jnp.flip(out_y[:, 2:4], axis=-1)
            wh_y = jnp.transpose(out_y[:, 1].reshape(Bn, Din, Ww, Hh), (0, 1, 3, 2)).reshape(Bn, Din, L)
            invwh_y = jnp.transpose(inv_y[:, 1].reshape(Bn, Din, Ww, Hh), (0, 1, 3, 2)).reshape(Bn, Din, L)
            y = out_y[:, 0] + inv_y[:, 0] + wh_y + invwh_y
            y = jnp.transpose(y, (0, 2, 1)).reshape(Bn, Hh, Ww, Din)
            mu = jnp.mean(y, axis=-1, keepdims=True)
            var = jnp.mean(jnp.square(y - mu), axis=-1, keepdims=True)
            y = (y - mu) * jax.lax.rsqrt(var + 1e-05) * out_norm_w + out_norm_b
            y = y * jax.nn.silu(z)
            return jnp.einsum('bhwd,cd->bhwc', y, out_proj_w)
        key = jax.random.key(seed)
        ks = jax.random.split(key, 8)
        x = jax.random.normal(ks[0], (B, H, W, C), jnp.float32)
        in_proj_w = jax.random.normal(ks[1], (2 * DIN, C), jnp.float32) * 0.02
        conv_w = jax.random.normal(ks[2], (DIN, 1, DCONV, DCONV), jnp.float32) * 0.1
        conv_b = jax.random.normal(ks[3], (DIN,), jnp.float32) * 0.02
        x_proj_weight = jax.random.normal(ks[4], (K, DTR + 2 * DSTATE, DIN), jnp.float32) * 0.02
        dt_projs_weight = jax.random.normal(ks[5], (K, DIN, DTR), jnp.float32) * DTR ** (-0.5)
        dt_projs_bias = jax.random.normal(ks[6], (K, DIN), jnp.float32) * 0.5 - 4.0
        A_logs = jnp.tile(jnp.log(jnp.arange(1, DSTATE + 1, dtype=jnp.float32))[None, :], (K * DIN, 1))
        Ds = jnp.ones((K * DIN,), jnp.float32)
        out_norm_w = jnp.ones((DIN,), jnp.float32)
        out_norm_b = jnp.zeros((DIN,), jnp.float32)
        out_proj_w = jax.random.normal(ks[7], (C, DIN), jnp.float32) * 0.02
        return {'x': x, 'in_proj_w': in_proj_w, 'conv_w': conv_w, 'conv_b': conv_b, 'x_proj_weight': x_proj_weight, 'dt_projs_weight': dt_projs_weight, 'dt_projs_bias': dt_projs_bias, 'A_logs': A_logs, 'Ds': Ds, 'out_norm_w': out_norm_w, 'out_norm_b': out_norm_b, 'out_proj_w': out_proj_w}
    _L1_conv_all = _L1_conv_setup()
    _L1_conv_in = {k: v for k, v in _L1_conv_all.items() if k in ('in_proj_w', 'conv_w', 'conv_b', 'x_proj_weight', 'dt_projs_weight', 'dt_projs_bias', 'A_logs', 'Ds', 'out_norm_w', 'out_norm_b', 'out_proj_w', )}
    del _L1_conv_all

    def _L2_conv_setup():
        import jax, jax.numpy as jnp
        import numpy as np
        B, H, W, C = (32, 112, 112, 192)
        KH = KW = 3
        key = jax.random.key(seed)
        k1, k2 = jax.random.split(key)
        x = jax.random.normal(k1, (B, H, W, C), dtype=jnp.float32)
        w = jax.random.normal(k2, (KH, KW, 1, C), dtype=jnp.float32) * 0.1
        b = jnp.zeros((C,), dtype=jnp.float32)
        return {'x': x, 'w': w, 'b': b}
    _L2_conv_all = _L2_conv_setup()
    _L2_conv_in = {k: v for k, v in _L2_conv_all.items() if k in ('w', 'b', )}
    del _L2_conv_all

    def _L3_conv_setup():
        import jax, jax.numpy as jnp
        import numpy as np
        B, H, W, C = (32, 112, 112, 192)
        KH = KW = 3
        key = jax.random.key(seed)
        k1, k2 = jax.random.split(key)
        x = jax.random.normal(k1, (B, H, W, C), dtype=jnp.float32)
        w = jax.random.normal(k2, (KH, KW, 1, C), dtype=jnp.float32) * 0.1
        b = jnp.zeros((C,), dtype=jnp.float32)
        return {'x': x, 'w': w, 'b': b}
    _L3_conv_all = _L3_conv_setup()
    _L3_conv_in = {k: v for k, v in _L3_conv_all.items() if k in ('w', 'b', )}
    del _L3_conv_all

    return {
        "x": x,
        "L0_conv_cpe1_w": _L0_conv_in["cpe1_w"],
        "L0_conv_cpe1_b": _L0_conv_in["cpe1_b"],
        "L0_conv_ln1_w": _L0_conv_in["ln1_w"],
        "L0_conv_ln1_b": _L0_conv_in["ln1_b"],
        "L0_conv_in_proj_w": _L0_conv_in["in_proj_w"],
        "L0_conv_conv1d_w": _L0_conv_in["conv1d_w"],
        "L0_conv_conv1d_b": _L0_conv_in["conv1d_b"],
        "L0_conv_dt_bias": _L0_conv_in["dt_bias"],
        "L0_conv_A_log": _L0_conv_in["A_log"],
        "L0_conv_D_skip": _L0_conv_in["D_skip"],
        "L0_conv_rms_w": _L0_conv_in["rms_w"],
        "L0_conv_out_proj_w": _L0_conv_in["out_proj_w"],
        "L0_conv_cpe2_w": _L0_conv_in["cpe2_w"],
        "L0_conv_cpe2_b": _L0_conv_in["cpe2_b"],
        "L0_conv_ln2_w": _L0_conv_in["ln2_w"],
        "L0_conv_ln2_b": _L0_conv_in["ln2_b"],
        "L0_conv_fc1_w": _L0_conv_in["fc1_w"],
        "L0_conv_fc1_b": _L0_conv_in["fc1_b"],
        "L0_conv_fc2_w": _L0_conv_in["fc2_w"],
        "L0_conv_fc2_b": _L0_conv_in["fc2_b"],
        "L1_conv_in_proj_w": _L1_conv_in["in_proj_w"],
        "L1_conv_conv_w": _L1_conv_in["conv_w"],
        "L1_conv_conv_b": _L1_conv_in["conv_b"],
        "L1_conv_x_proj_weight": _L1_conv_in["x_proj_weight"],
        "L1_conv_dt_projs_weight": _L1_conv_in["dt_projs_weight"],
        "L1_conv_dt_projs_bias": _L1_conv_in["dt_projs_bias"],
        "L1_conv_A_logs": _L1_conv_in["A_logs"],
        "L1_conv_Ds": _L1_conv_in["Ds"],
        "L1_conv_out_norm_w": _L1_conv_in["out_norm_w"],
        "L1_conv_out_norm_b": _L1_conv_in["out_norm_b"],
        "L1_conv_out_proj_w": _L1_conv_in["out_proj_w"],
        "L2_conv_w": _L2_conv_in["w"],
        "L2_conv_b": _L2_conv_in["b"],
        "L3_conv_w": _L3_conv_in["w"],
        "L3_conv_b": _L3_conv_in["b"],
    }

def reference(x, L0_conv_cpe1_w, L0_conv_cpe1_b, L0_conv_ln1_w, L0_conv_ln1_b, L0_conv_in_proj_w, L0_conv_conv1d_w, L0_conv_conv1d_b, L0_conv_dt_bias, L0_conv_A_log, L0_conv_D_skip, L0_conv_rms_w, L0_conv_out_proj_w, L0_conv_cpe2_w, L0_conv_cpe2_b, L0_conv_ln2_w, L0_conv_ln2_b, L0_conv_fc1_w, L0_conv_fc1_b, L0_conv_fc2_w, L0_conv_fc2_b, L1_conv_in_proj_w, L1_conv_conv_w, L1_conv_conv_b, L1_conv_x_proj_weight, L1_conv_dt_projs_weight, L1_conv_dt_projs_bias, L1_conv_A_logs, L1_conv_Ds, L1_conv_out_norm_w, L1_conv_out_norm_b, L1_conv_out_proj_w, L2_conv_w, L2_conv_b, L3_conv_w, L3_conv_b):
    import jax
    import jax.numpy as jnp
    def _L0_conv_ref(x, cpe1_w, cpe1_b, ln1_w, ln1_b, in_proj_w, conv1d_w, conv1d_b, dt_bias, A_log, D_skip, rms_w, out_proj_w, cpe2_w, cpe2_b, ln2_w, ln2_b, fc1_w, fc1_b, fc2_w, fc2_b):
        import jax, jax.numpy as jnp
        import numpy as np
        DIM = 192
        NH = 6
        EXP = 2
        DSTATE = 64
        NG = 1
        CHUNK = 256
        DCONV = 4
        DIN = DIM * EXP
        HD = DIN // NH
        CONVDIM = DIN + 2 * NG * DSTATE
        DPROJ = 2 * DIN + 2 * NG * DSTATE + NH
        B_, H_, W_ = (8, 64, 64)

        def layernorm(x, w, b, eps=1e-05):
            mu = jnp.mean(x, -1, keepdims=True)
            v = jnp.mean(jnp.square(x - mu), -1, keepdims=True)
            return (x - mu) * jax.lax.rsqrt(v + eps) * w + b

        def dwconv2d(x_nchw, w, b):
            y = jax.lax.conv_general_dilated(x_nchw, w, (1, 1), 'SAME', feature_group_count=x_nchw.shape[1], dimension_numbers=('NCHW', 'OIHW', 'NCHW'))
            return y + b[None, :, None, None]

        def causal_conv1d(x, w, b):
            K = w.shape[1]
            L = x.shape[1]
            xp = jnp.pad(x, ((0, 0), (K - 1, 0), (0, 0)))
            y = sum((xp[:, k:k + L, :] * w[:, k] for k in range(K)))
            return y + b

        def ssd(x, dt, A, Bm, Cm, chunk):
            b, l, h, p = x.shape
            n = Bm.shape[-1]
            nc = l // chunk
            x = x.reshape(b, nc, chunk, h, p)
            dt = dt.reshape(b, nc, chunk, h)
            Bm = Bm.reshape(b, nc, chunk, n)
            Cm = Cm.reshape(b, nc, chunk, n)
            dA = dt * A
            dA_cs = jnp.cumsum(dA, axis=2)
            seg = dA_cs[:, :, :, None, :] - dA_cs[:, :, None, :, :]
            mask = jnp.tril(jnp.ones((chunk, chunk), bool))
            seg = jnp.where(mask[None, None, :, :, None], seg, -1e+30)
            scores = jnp.einsum('bcin,bcjn->bcij', Cm, Bm)[..., None] * jnp.exp(seg) * dt[:, :, None, :, :]
            y = jnp.einsum('bcijh,bcjhp->bcihp', scores, x)
            decay_last = jnp.exp(dA_cs[:, :, -1:, :] - dA_cs)
            states = jnp.einsum('bcjn,bcjh,bcjhp->bchnp', Bm, dt * decay_last, x)
            chunk_decay = jnp.exp(dA_cs[:, :, -1, :])

            def step(carry, inp):
                s, cd = inp
                new = carry * cd[:, :, None, None] + s
                return (new, carry)
            init = jnp.zeros((b, h, n, p), x.dtype)
            _, prev = jax.lax.scan(step, init, (states.swapaxes(0, 1), chunk_decay.swapaxes(0, 1)))
            prev = prev.swapaxes(0, 1)
            y = y + jnp.einsum('bcin,bchnp,bcih->bcihp', Cm, prev, jnp.exp(dA_cs))
            return y.reshape(b, l, h, p)
        B, H, W, C = x.shape
        L = H * W
        xc = jnp.transpose(x, (0, 3, 1, 2))
        c1 = jnp.transpose(dwconv2d(xc, cpe1_w, cpe1_b).reshape(B, C, L), (0, 2, 1))
        xs = x.reshape(B, L, C) + c1
        short = xs
        h = layernorm(xs, ln1_w, ln1_b)
        zxbcdt = h @ in_proj_w.T
        z = zxbcdt[..., :DIN]
        xBC = zxbcdt[..., DIN:DIN + CONVDIM]
        dt = jax.nn.softplus(zxbcdt[..., DIN + CONVDIM:] + dt_bias)
        xBC = jax.nn.silu(causal_conv1d(xBC, conv1d_w, conv1d_b))
        xm = xBC[..., :DIN].reshape(B, L, NH, HD)
        Bm = xBC[..., DIN:DIN + DSTATE]
        Cm = xBC[..., DIN + DSTATE:]
        A = -jnp.exp(A_log)
        y = ssd(xm, dt, A, Bm, Cm, CHUNK)
        y = y + xm * D_skip[None, None, :, None]
        y = y.reshape(B, L, DIN) * jax.nn.silu(z)
        y = y * jax.lax.rsqrt(jnp.mean(y * y, -1, keepdims=True) + 1e-05) * rms_w
        attn = y @ out_proj_w.T
        x2 = short + attn
        c2 = dwconv2d(jnp.transpose(x2.reshape(B, H, W, C), (0, 3, 1, 2)), cpe2_w, cpe2_b)
        x2 = x2 + jnp.transpose(c2.reshape(B, C, L), (0, 2, 1))
        h2 = layernorm(x2, ln2_w, ln2_b)
        m = jax.nn.gelu(h2 @ fc1_w.T + fc1_b, approximate=False) @ fc2_w.T + fc2_b
        return (x2 + m).reshape(B, H, W, C)

    def _L1_conv_ref(x, in_proj_w, conv_w, conv_b, x_proj_weight, dt_projs_weight, dt_projs_bias, A_logs, Ds, out_norm_w, out_norm_b, out_proj_w):
        import jax, jax.numpy as jnp
        import numpy as np
        B, H, W, C = (4, 64, 64, 192)
        EXPAND, DSTATE, DCONV = (2, 16, 3)
        DIN = EXPAND * C
        DTR = -(-C // 16)
        K = 4

        def _ss2d(x, in_proj_w, conv_w, conv_b, x_proj_weight, dt_projs_weight, dt_projs_bias, A_logs, Ds, out_norm_w, out_norm_b, out_proj_w):
            Bn, Hh, Ww, Cm = x.shape
            L = Hh * Ww
            Din = conv_w.shape[0]
            N = A_logs.shape[-1]
            R = dt_projs_weight.shape[-1]
            xz = jnp.einsum('bhwc,oc->bhwo', x, in_proj_w)
            xa, z = jnp.split(xz, 2, axis=-1)
            xc = jnp.transpose(xa, (0, 3, 1, 2))
            xc = jax.lax.conv_general_dilated(xc, conv_w, (1, 1), 'SAME', feature_group_count=Din, dimension_numbers=('NCHW', 'OIHW', 'NCHW')) + conv_b[None, :, None, None]
            xc = jax.nn.silu(xc)
            x_flat = xc.reshape(Bn, Din, L)
            x_trans = jnp.transpose(xc, (0, 1, 3, 2)).reshape(Bn, Din, L)
            x_hwwh = jnp.stack([x_flat, x_trans], axis=1)
            xs = jnp.concatenate([x_hwwh, jnp.flip(x_hwwh, axis=-1)], axis=1)
            x_dbl = jnp.einsum('bkdl,kcd->bkcl', xs, x_proj_weight)
            dts, Bs, Cs = jnp.split(x_dbl, [R, R + N], axis=2)
            dts = jnp.einsum('bkrl,kdr->bkdl', dts, dt_projs_weight)
            A = -jnp.exp(A_logs).reshape(4, Din, N)
            delta = jax.nn.softplus(dts + dt_projs_bias[None, :, :, None])

            def step(h, inp):
                u_l, d_l, B_l, C_l = inp
                dA = jnp.exp(d_l[..., None] * A)
                dBu = d_l[..., None] * B_l[:, :, None, :] * u_l[..., None]
                h = dA * h + dBu
                y = jnp.sum(h * C_l[:, :, None, :], axis=-1)
                return (h, y)
            inputs = (jnp.moveaxis(xs, -1, 0), jnp.moveaxis(delta, -1, 0), jnp.moveaxis(Bs, -1, 0), jnp.moveaxis(Cs, -1, 0))
            h0 = jnp.zeros((Bn, 4, Din, N), xs.dtype)
            _, ys = jax.lax.scan(step, h0, inputs)
            out_y = jnp.moveaxis(ys, 0, -1) + xs * Ds.reshape(4, Din)[None, :, :, None]
            inv_y = jnp.flip(out_y[:, 2:4], axis=-1)
            wh_y = jnp.transpose(out_y[:, 1].reshape(Bn, Din, Ww, Hh), (0, 1, 3, 2)).reshape(Bn, Din, L)
            invwh_y = jnp.transpose(inv_y[:, 1].reshape(Bn, Din, Ww, Hh), (0, 1, 3, 2)).reshape(Bn, Din, L)
            y = out_y[:, 0] + inv_y[:, 0] + wh_y + invwh_y
            y = jnp.transpose(y, (0, 2, 1)).reshape(Bn, Hh, Ww, Din)
            mu = jnp.mean(y, axis=-1, keepdims=True)
            var = jnp.mean(jnp.square(y - mu), axis=-1, keepdims=True)
            y = (y - mu) * jax.lax.rsqrt(var + 1e-05) * out_norm_w + out_norm_b
            y = y * jax.nn.silu(z)
            return jnp.einsum('bhwd,cd->bhwc', y, out_proj_w)
        return _ss2d(x, in_proj_w, conv_w, conv_b, x_proj_weight, dt_projs_weight, dt_projs_bias, A_logs, Ds, out_norm_w, out_norm_b, out_proj_w)

    def _L2_conv_ref(x, w, b):
        import jax, jax.numpy as jnp
        import numpy as np
        B, H, W, C = (32, 112, 112, 192)
        KH = KW = 3
        out = jax.lax.conv_general_dilated(x, w, window_strides=(1, 1), padding='SAME', rhs_dilation=(1, 1), dimension_numbers=('NHWC', 'HWIO', 'NHWC'), feature_group_count=C)
        return out + b

    def _L3_conv_ref(x, w, b):
        import jax, jax.numpy as jnp
        import numpy as np
        B, H, W, C = (32, 112, 112, 192)
        KH = KW = 3
        out = jax.lax.conv_general_dilated(x, w, window_strides=(1, 1), padding='SAME', rhs_dilation=(1, 1), dimension_numbers=('NHWC', 'HWIO', 'NHWC'), feature_group_count=C)
        return out + b

    def _gn(v, G=32, eps=1e-5):
        B_, H_, W_, C_ = v.shape
        g = v.reshape(B_, H_, W_, G, C_ // G)
        m = jnp.mean(g, axis=(1, 2, 4), keepdims=True)
        s = jnp.var(g, axis=(1, 2, 4), keepdims=True)
        return ((g - m) / jnp.sqrt(s + eps)).reshape(v.shape)

    def _ln_c(v, eps=1e-6):
        m = jnp.mean(v, axis=-1, keepdims=True)
        s = jnp.var(v, axis=-1, keepdims=True)
        return (v - m) / jnp.sqrt(s + eps)

    def _ln_t(v, eps=1e-5):
        m = jnp.mean(v, axis=-1, keepdims=True)
        s = jnp.var(v, axis=-1, keepdims=True)
        return (v - m) / jnp.sqrt(s + eps)

    def _to_tokens(v):
        B_, H_, W_, C_ = v.shape
        return v.reshape(B_, H_ * W_, C_)
    def _from_tokens(t, like):
        return t.reshape(like.shape)

    x = x + _L0_conv_ref(_gn(x), L0_conv_cpe1_w, L0_conv_cpe1_b, L0_conv_ln1_w, L0_conv_ln1_b, L0_conv_in_proj_w, L0_conv_conv1d_w, L0_conv_conv1d_b, L0_conv_dt_bias, L0_conv_A_log, L0_conv_D_skip, L0_conv_rms_w, L0_conv_out_proj_w, L0_conv_cpe2_w, L0_conv_cpe2_b, L0_conv_ln2_w, L0_conv_ln2_b, L0_conv_fc1_w, L0_conv_fc1_b, L0_conv_fc2_w, L0_conv_fc2_b)
    x = x + _L1_conv_ref(_gn(x), L1_conv_in_proj_w, L1_conv_conv_w, L1_conv_conv_b, L1_conv_x_proj_weight, L1_conv_dt_projs_weight, L1_conv_dt_projs_bias, L1_conv_A_logs, L1_conv_Ds, L1_conv_out_norm_w, L1_conv_out_norm_b, L1_conv_out_proj_w)
    x = x + _L2_conv_ref(_gn(x), L2_conv_w, L2_conv_b)
    x = x + _L3_conv_ref(_gn(x), L3_conv_w, L3_conv_b)
    return x


_drawn_inputs = setup_inputs


def setup_inputs(seed=0):
    import zlib

    import numpy as np

    out = dict(_drawn_inputs(seed))
    spreads = {'L0_conv_cpe1_b': (0.0, 0.1),
     'L0_conv_ln1_w': (1.0, 0.2),
     'L0_conv_ln1_b': (0.0, 0.442),
     'L0_conv_conv1d_b': (0.0, 0.1),
     'L0_conv_D_skip': (1.0, 0.6),
     'L0_conv_rms_w': (1.0, 0.2),
     'L0_conv_cpe2_b': (0.0, 0.1),
     'L0_conv_ln2_w': (1.0, 0.6),
     'L0_conv_ln2_b': (0.0, 0.8),
     'L0_conv_fc1_b': (0.0, 0.535),
     'L0_conv_fc2_b': (0.0, 0.1),
     'L1_conv_Ds': (1.0, 0.6),
     'L1_conv_out_norm_w': (1.0, 0.6),
     'L1_conv_out_norm_b': (0.0, 0.8),
     'L2_conv_b': (0.0, 0.1),
     'L3_conv_b': (0.0, 0.1)}
    factors = {'L0_conv_dt_bias': 8.0,
     'L0_conv_A_log': 8.0,
     'L1_conv_conv_b': 8.0,
     'L1_conv_x_proj_weight': 8.0,
     'L1_conv_dt_projs_weight': 8.0,
     'L1_conv_dt_projs_bias': 8.0,
     'L1_conv_A_logs': 8.0}
    for name, (base, spread) in spreads.items():
        noise = np.random.default_rng([zlib.crc32(name.encode()), seed]).standard_normal(out[name].shape)
        drawn = base * np.exp(spread * noise) if base else spread * noise
        out[name] = jnp.asarray(drawn.astype(out[name].dtype))
    for name, factor in factors.items():
        out[name] = (out[name] * factor).astype(out[name].dtype)
    return out
```

```python
from contextlib import ExitStack

import concourse.bass as bass
from concourse import mybir

F32 = mybir.dt.float32
BF16 = mybir.dt.bfloat16
ALU = mybir.AluOpType
ACT = mybir.ActivationFunctionType

B, H, W, C = 8, 64, 64, 192
L = H * W
P = 96
NH = C // P
GROUP = 6
T = 512
NT = L // T
ROWS = 16
D2 = 2 * C
N2 = D2 // 128
HEADS, HD, DS = 6, 64, 64
Q = 128
NQ = T // Q
DTR, NS, K4 = 12, 16, 4
UNITS = N2 * NS
DIN0 = D2 + HEADS
MLP = 4 * C
NM = MLP // 128
PE_TAPS = (4, 1, 3, 5, 7)
DVE_TAPS = (0, 2, 6, 8)
SLOT = L
SLOTS = 12
EXTRA = 2048


def window(tap, r0, r1):
    dy, dx = tap // 3 - 1, tap % 3 - 1
    ya, yb = max(r0, -dy), min(r1, H - dy)
    xa, xb = max(0, -dx), min(W, W - dx)
    return (ya, yb, xa, xb), (ya + dy, yb + dy, xa + dx, xb + dx)


class Stage:

    def __init__(self, nc, *names):
        self.nc, self.names, self.stack = nc, names, ExitStack()

    def __enter__(self):
        self.sems = [self.stack.enter_context(self.nc.semaphore(n)) for n in self.names]
        return self.sems

    def __exit__(self, *e):
        if e[0] is None:
            for s in self.sems:
                self.nc.gpsimd.sem_clear(s)
            self.nc.all_engine_barrier()
        self.stack.close()


class Chip:

    def __init__(self, nc, ctx):
        def sb(name, shape, dt=F32):
            return ctx.enter_context(nc.sbuf_tensor(name, shape, dt))

        self.nc = nc
        self.arena = sb("arena", [128, SLOTS * SLOT + EXTRA])
        self.ps = ctx.enter_context(nc.psum_tensor("ps", [128, 8, T], F32))
        self.ident = sb("ident", [128, 128])
        self.sel = sb("sel", [P, 32], BF16)
        self.eps = sb("eps", [128, 1])
        self.gn_mean = sb("gn_mean", [P, NH])
        self.gn_rstd = sb("gn_rstd", [P, NH])
        self.hist = sb("hist", [128, 5, 3])
        self.top = 0

    def slots(self, first, n, parts=128):
        return self.arena[0:parts, first * SLOT:(first + n) * SLOT].rearrange("p (t l) -> p t l", t=n)

    def start(self, slot):
        self.top = slot * SLOT

    def take(self, *shape, parts=128):
        n = 1
        for x in shape:
            n *= x
        a = self.arena[0:parts, self.top:self.top + n]
        self.top += n
        assert self.top <= SLOTS * SLOT + EXTRA, self.top
        if len(shape) == 2:
            return a.rearrange("p (a b) -> p a b", a=shape[0])
        if len(shape) == 3:
            return a.rearrange("p (a b c) -> p a b c", a=shape[0], b=shape[1])
        return a


def constants(m):
    nc = m.nc
    with Stage(nc, "filled", "cut") as (filled, cut), nc.Block() as block:
        @block.gpsimd
        def _(pool):
            nc.gpsimd.memset(m.ident[:, :], 0.0).then_inc(filled, 1)
            nc.gpsimd.memset(m.sel[:, :], 0.0).then_inc(filled, 1)
            nc.gpsimd.memset(m.eps[:, :], 1e-5)
            pool.wait_ge(filled, 2)
            nc.gpsimd.affine_select(out=m.ident[:, :], in_=m.ident[:, :], compare_op=ALU.not_equal, fill=1.0,
                                    base=0, pattern=[[-1, 128]], channel_multiplier=1)
            for i in range(3):
                nc.gpsimd.affine_select(out=m.sel[:, :], in_=m.sel[:, :], compare_op=ALU.not_equal, fill=1.0,
                                        base=-32 * i, pattern=[[-1, 32]], channel_multiplier=1).then_inc(cut, 1)
                pool.wait_ge(cut, i + 1)


def group_norm(m, src, dst, load=None):
    nc = m.nc
    m.start(10)
    stats = m.take(NH, 8 * 6, parts=P)
    mv = m.take(NH, 2, parts=P)
    dev = m.take(NH, parts=P)
    group = m.take(P, parts=P)
    names = ("loaded_0", "loaded_1", "group_set", "stats_done", "mean_mm", "var_in", "var_mm", "chain", "rstd_in", "rstd_out")
    with Stage(nc, *names) as (*loaded, group_set, stats_done, mean_mm, var_in, var_mm, chain, rstd_in, rstd_out), \
            nc.Block() as block:
        if load is not None:
            @block.sync
            def _(sp):
                for h in range(NH):
                    sp.dma_start(src[:, h, :], load[:, h, :]).then_inc(loaded[h], 16)

        @block.gpsimd
        def _(pool):
            nc.gpsimd.memset(group, 1.0 / GROUP).then_inc(group_set, 1)
            pool.wait_ge(group_set, 1)
            g3 = group.rearrange("p (g c) -> p g c", c=GROUP)
            nc.gpsimd.affine_select(out=g3, in_=g3, compare_op=ALU.is_ge, fill=0.0, base=0,
                                    pattern=[[-GROUP, P // GROUP], [0, GROUP]], channel_multiplier=1).then_inc(group_set, 1)
            pool.wait_ge(group_set, 2)
            nc.gpsimd.affine_select(out=g3, in_=g3, compare_op=ALU.is_ge, fill=0.0, base=GROUP - 1,
                                    pattern=[[GROUP, P // GROUP], [0, GROUP]], channel_multiplier=-1).then_inc(group_set, 1)

        @block.vector
        def _(dve):
            n = 0

            def link(ins):
                nonlocal n
                n += 1
                ins.then_inc(chain, 1)
                dve.wait_ge(chain, n)

            for h in range(NH):
                if load is not None:
                    dve.wait_ge(loaded[h], 16)
                for i in range(8):
                    ins = nc.vector.bn_stats(stats[:, h, 6 * i:6 * i + 6], src[:, h, i * T:(i + 1) * T])
                    if i == 7:
                        link(ins)
                link(nc.vector.bn_aggr(mv[:, h, :], stats[:, h, :]))
            nc.vector.tensor_copy(dev, mv[:, :, 0]).then_inc(stats_done, 1)
            dve.wait_ge(mean_mm, 1)
            link(nc.vector.tensor_copy(m.gn_mean[:, :], m.ps[0:P, 0, 0:NH]))
            link(nc.vector.tensor_tensor(dev, dev, m.gn_mean[:, :], ALU.subtract))
            link(nc.vector.tensor_tensor(dev, dev, dev, ALU.mult))
            nc.vector.tensor_tensor(dev, dev, mv[:, :, 1], ALU.add).then_inc(var_in, 1)
            dve.wait_ge(var_mm, 1)
            nc.vector.tensor_scalar(m.gn_rstd[:, :], m.ps[0:P, 1, 0:NH], 1e-5, None, ALU.add).then_inc(rstd_in, 1)
            dve.wait_ge(rstd_out, 1)
            link(nc.vector.reciprocal(m.gn_rstd[:, :], m.gn_rstd[:, :]))
            for h in range(NH):
                nc.vector.tensor_scalar(dst[:, h, :], src[:, h, :], m.gn_mean[:, h:h + 1], m.gn_rstd[:, h:h + 1],
                                        ALU.subtract, ALU.mult)

        @block.scalar
        def _(act):
            act.wait_ge(rstd_in, 1)
            nc.scalar.activation(m.gn_rstd[:, :], m.gn_rstd[:, :], ACT.Sqrt).then_inc(rstd_out, 1)

        @block.tensor
        def _(pe):
            pe.wait_ge(group_set, 3)
            pe.wait_ge(stats_done, 1)
            nc.tensor.matmul(m.ps[0:P, 0, 0:NH], group, dev, start=True, stop=True).then_inc(mean_mm, 1)
            pe.wait_ge(var_in, 1)
            nc.tensor.matmul(m.ps[0:P, 1, 0:NH], group, dev, start=True, stop=True).then_inc(var_mm, 1)


def conv3x3(m, src, dst, n, parts, weight, bias, own=False, residual=None, silu=False):
    nc = m.nc
    m.start(11 if n == NH else 0)
    w = m.take(n, 9, parts=parts)
    bcol = m.take(n, parts=parts)
    diag = m.take(n * len(PE_TAPS), parts, parts=parts)
    steps = [(t, r) for t in range(n) for r in range(0, H, ROWS)]
    src4 = src.rearrange("p t (h w) -> p t h w", w=W)
    dst4 = dst.rearrange("p t (h w) -> p t h w", w=W)
    with Stage(nc, "loaded", "centre", "diags", "taps_mm", "taken", "tapped", "summed") as \
            (loaded, centre, diags, taps_mm, taken, tapped, summed), nc.Block() as block:
        @block.sync
        def _(sp):
            sp.dma_start(w, weight.rearrange("(t p) k -> p t k", p=parts)).then_inc(loaded, 16)
            with nc.allow_non_contiguous_dma(reason="a few words a partition"):
                sp.dma_start(bcol, bias.rearrange("(t p) -> p t", p=parts)).then_inc(loaded, 16)

        @block.gpsimd
        def _(pool):
            pool.wait_ge(loaded, 32)
            if own:
                nc.gpsimd.tensor_scalar(w[:, :, 4:5], w[:, :, 4:5], 1.0, None, ALU.add).then_inc(centre, 1)
                pool.wait_ge(centre, 1)
            for t in range(n):
                for i, tap in enumerate(PE_TAPS):
                    ins = nc.gpsimd.tensor_scalar(diag[:, t * len(PE_TAPS) + i, :], m.ident[0:parts, 0:parts],
                                                  w[:, t, tap:tap + 1], None, ALU.mult)
                ins.then_inc(diags, 1)
            if residual is not None:
                for i, (t, r) in enumerate(steps):
                    pool.wait_ge(tapped, len(DVE_TAPS) * (i + 1))
                    cut = slice(r * W, (r + ROWS) * W)
                    nc.gpsimd.tensor_tensor(dst[:, t, cut], dst[:, t, cut], residual[:, t, cut], ALU.add)

        @block.tensor
        def _(pe):
            for i, (t, r) in enumerate(steps):
                if r == 0:
                    pe.wait_ge(diags, t + 1)
                if i >= 4:
                    pe.wait_ge(taken, i - 3)
                for half in range(2):
                    bank = (2 * i + half) % 8
                    r0 = r + 8 * half
                    out = m.ps[0:parts, bank, :].rearrange("p (h w) -> p h w", w=W)
                    for j, tap in enumerate(PE_TAPS):
                        (ya, yb, xa, xb), (sa, sb_, ca, cb) = window(tap, r0, r0 + 8)
                        ins = nc.tensor.matmul(out[:, ya - r0:yb - r0, xa:xb], diag[:, t * len(PE_TAPS) + j, :],
                                               src4[:, t, sa:sb_, ca:cb], start=(j == 0), stop=(j == len(PE_TAPS) - 1))
                ins.then_inc(taps_mm, 1)

        @block.scalar
        def _(act):
            act.wait_ge(loaded, 32)

            def finish(i):
                t, r = steps[i]
                act.wait_ge(tapped, len(DVE_TAPS) * (i + 1))
                cut = slice(r * W, (r + ROWS) * W)
                nc.scalar.activation(dst[:, t, cut], dst[:, t, cut], ACT.Silu, bias=bcol[:, t:t + 1])

            for i, (t, r) in enumerate(steps):
                act.wait_ge(taps_mm, i + 1)
                both = m.ps[0:parts, (2 * i) % 8:(2 * i) % 8 + 2, :]
                out = dst[:, t, r * W:(r + ROWS) * W].rearrange("p (a b) -> p a b", a=2)
                if silu:
                    nc.scalar.copy(out, both).then_inc(taken, 1)
                    if i >= 2:
                        finish(i - 2)
                else:
                    nc.scalar.activation(out, both, ACT.Identity, bias=bcol[:, t:t + 1]).then_inc(taken, 1)
            if silu:
                finish(len(steps) - 2)
                finish(len(steps) - 1)

        @block.vector
        def _(dve):
            dve.wait_ge(loaded, 32)
            for i, (t, r) in enumerate(steps):
                dve.wait_ge(taken, i + 1)
                for j, tap in enumerate(DVE_TAPS):
                    (ya, yb, xa, xb), (sa, sb_, ca, cb) = window(tap, r, r + ROWS)
                    o = dst4[:, t, ya:yb, xa:xb]
                    if j:
                        dve.wait_ge(tapped, len(DVE_TAPS) * i + j)
                    nc.vector.scalar_tensor_tensor(o, src4[:, t, sa:sb_, ca:cb], w[:, t, tap:tap + 1], o,
                                                   ALU.mult, ALU.add).then_inc(tapped, 1)


class LayerNorm:

    NAMES = ("ln_mean", "ln_centred", "ln_squared", "ln_var", "ln_log", "ln_rstd", "ln_scaled", "ln_out")

    def __init__(self, m, n, parts, wcol, bcol):
        self.m, self.n, self.parts, self.wcol, self.bcol = m, n, parts, wcol, bcol
        self.xc = m.take(n, T, parts=parts)
        self.sq = m.take(n, T, parts=parts)
        self.rstd = m.take(T, parts=parts)
        self.mean_of = m.take(parts, parts=parts)

    def constants(self):
        return self.m.nc.vector.memset(self.mean_of, 1.0 / (self.n * self.parts))

    def pe(self, pe, s, x):
        nc, ps = self.m.nc, self.m.ps
        for t in range(self.n):
            ins = nc.tensor.matmul(ps[0:self.parts, 0, :], self.mean_of, x[:, t, :], start=(t == 0), stop=(t == self.n - 1))
        ins.then_inc(s["ln_mean"], 1)
        for t in range(self.n):
            pe.wait_ge(s["ln_squared"], t + 1)
            ins = nc.tensor.matmul(ps[0:self.parts, 1, :], self.mean_of, self.sq[:, t, :], start=(t == 0), stop=(t == self.n - 1))
        ins.then_inc(s["ln_var"], 1)

    def dve(self, dve, s, x):
        nc, ps = self.m.nc, self.m.ps
        dve.wait_ge(s["ln_mean"], 1)
        for t in range(self.n):
            nc.vector.tensor_tensor(self.xc[:, t, :], x[:, t, :], ps[0:self.parts, 0, :], ALU.subtract).then_inc(s["ln_centred"], 1)
        dve.wait_ge(s["ln_rstd"], 1)
        dve.wait_ge(s["ln_centred"], self.n)
        for t in range(self.n):
            nc.vector.tensor_tensor(self.xc[:, t, :], self.xc[:, t, :], self.rstd, ALU.mult).then_inc(s["ln_scaled"], 1)

    def act(self, act, s, out):
        nc, ps = self.m.nc, self.m.ps
        for t in range(self.n):
            act.wait_ge(s["ln_centred"], t + 1)
            nc.scalar.square(self.sq[:, t, :], self.xc[:, t, :]).then_inc(s["ln_squared"], 1)
        act.wait_ge(s["ln_var"], 1)
        nc.scalar.activation(self.rstd, ps[0:self.parts, 1, :], ACT.Ln, bias=self.m.eps[0:self.parts, :]).then_inc(s["ln_log"], 1)
        act.wait_ge(s["ln_log"], 1)
        nc.scalar.activation(self.rstd, self.rstd, ACT.Exp, scale=-0.5).then_inc(s["ln_rstd"], 1)
        for t in range(self.n):
            act.wait_ge(s["ln_scaled"], t + 1)
            nc.scalar.activation(out[:, t, :], self.xc[:, t, :], ACT.Identity, scale=self.wcol[:, t:t + 1],
                                 bias=self.bcol[:, t:t + 1]).then_inc(s["ln_out"], 1)


def columns(vector, parts):
    return vector.rearrange("(t p) -> p t", p=parts)


def load_all(nc, loads, landed, values=None):
    with Stage(nc, "landed") as (landed,), nc.Block() as block:
        @block.sync
        def _(sp):
            with nc.allow_non_contiguous_dma(reason="columns of small vectors"):
                for dst, src in loads:
                    sp.dma_start(dst, src).then_inc(landed, 16)
            sp.wait_ge(landed, 16 * len(loads))


def mlp(m, x2, x, a):
    nc = m.nc
    m.start(4)
    w1 = m.take(NH, MLP, parts=P)
    w2 = m.take(NM, C)
    b1 = m.take(NM)
    cols = m.take(3, NH, parts=P)
    ln = LayerNorm(m, NH, P, cols[:, 0, :], cols[:, 1, :])
    xin = m.take(NH, T, parts=P)
    h = m.take(NH, T, parts=P)
    g = m.take(NM, T)
    load_all(nc, [(w1, a["fc1_w"].rearrange("(t p) o -> p t o", p=P)), (w2, a["fc2_w"].rearrange("(t p) o -> p t o", p=128)),
                  (b1, columns(a["fc1_b"], 128)), (cols[:, 0, :], columns(a["ln2_w"], P)),
                  (cols[:, 1, :], columns(a["ln2_b"], P)), (cols[:, 2, :], columns(a["fc2_b"], P))], None)
    with nc.Fori(0, NT) as s:
        names = ("taken", "ones_set", "fc1_mm", "gelu_done", "fc2_mm", "added") + LayerNorm.NAMES
        with Stage(nc, *names) as sems, nc.Block() as block:
            at = dict(zip(names, sems))
            taken, ones_set, fc1_mm, gelu_done, fc2_mm, added = sems[:6]

            @block.scalar
            def _(act):
                nc.scalar.copy(xin, x2[:, :, bass.ds(s * T, T)]).then_inc(taken, 1)
                ln.act(act, at, h)
                for o in range(NM):
                    act.wait_ge(fc1_mm, o + 1)
                    nc.scalar.activation(g[:, o, :], m.ps[:, 2 + o % 4, :], ACT.Gelu, bias=b1[:, o:o + 1]).then_inc(gelu_done, 1)

            @block.tensor
            def _(pe):
                pe.wait_ge(taken, 1)
                pe.wait_ge(ones_set, 1)
                ln.pe(pe, at, xin)
                pe.wait_ge(at["ln_out"], NH)
                for o in range(NM):
                    if o >= 4:
                        pe.wait_ge(gelu_done, o - 3)
                    for t in range(NH):
                        ins = nc.tensor.matmul(m.ps[:, 2 + o % 4, :], w1[:, t, o * 128:(o + 1) * 128], h[:, t, :],
                                               start=(t == 0), stop=(t == NH - 1))
                    ins.then_inc(fc1_mm, 1)
                for c in range(NH):
                    for o in range(NM):
                        pe.wait_ge(gelu_done, o + 1)
                        ins = nc.tensor.matmul(m.ps[0:P, 6 + c, :], w2[:, o, c * P:(c + 1) * P], g[:, o, :],
                                               start=(o == 0), stop=(o == NM - 1))
                    ins.then_inc(fc2_mm, 1)

            @block.vector
            def _(dve):
                ln.constants().then_inc(ones_set, 1)
                dve.wait_ge(taken, 1)
                ln.dve(dve, at, xin)
                for c in range(NH):
                    blk = x[:, c:c + 1, bass.ds(s * T, T)].rearrange("p a t -> p (a t)")
                    nc.vector.scalar_tensor_tensor(blk, xin[:, c, :], cols[:, 2, c:c + 1], blk, ALU.add, ALU.add).then_inc(added, 1)
                    dve.wait_ge(fc2_mm, c + 1)
                    dve.wait_ge(added, c + 1)
                    nc.vector.tensor_tensor(blk, m.ps[0:P, 6 + c, :], blk, ALU.add)


def ssd(m, xs, a):
    nc = m.nc
    m.start(2)
    w_zdt = m.take(NH, DIN0, parts=P)
    w_xbc = m.take(NH, D2 + 2 * DS, parts=P)
    w_out = m.take(N2, C)
    xb = m.take(5, 3 + T)
    xbc = m.take(5, T)
    assert m.top <= 4 * SLOT
    m.start(6)
    lncol = m.take(2, NH, parts=P)
    cw = m.take(5, 4)
    cb = m.take(5)
    rms = m.take(N2)
    dt_bias = m.take(HEADS)
    neg_a = m.take(HEADS)
    skip = m.take(HEADS)
    upto = m.take(Q)
    after = m.take(Q)
    ones = m.take(Q)
    state = m.take(D2, parts=DS)
    ln = LayerNorm(m, NH, P, lncol[:, 0, :], lncol[:, 1, :])
    xin = m.take(NH, T, parts=P)
    h = m.take(NH, T, parts=P)
    sz = m.take(NQ, D2)
    dtr = m.take(NQ * HEADS)
    dte = m.take(NQ * HEADS)
    dtw = m.take(NQ * HEADS)
    dtl = m.take(NQ * HEADS)
    dt = m.take(NQ * HEADS)
    da = m.take(NQ, HEADS)
    dec = m.take(3, NQ, HEADS)
    xtok = m.take(NQ, D2 + DS)
    xdt = m.take(NQ, D2)
    xdl = m.take(NQ, D2)
    r = m.take(2, HEADS * Q)
    e = m.take(2, HEADS * Q)
    cbm = m.take(2, Q)
    y = m.take(NQ, D2)
    ss = m.take(NQ)
    yt = m.take(N2, T)
    in_w = a["in_proj_w"].rearrange("(t p) o -> p t o", p=P)
    cwd = a["conv1d_w"]
    cbd = a["conv1d_b"].rearrange("(a c) -> a c", c=1)
    loads = [(w_zdt[:, :, 0:D2], in_w[:, :, 0:D2]), (w_zdt[:, :, D2:DIN0], in_w[:, :, 2 * D2 + 2 * DS:]),
             (w_xbc, in_w[:, :, D2:2 * D2 + 2 * DS]), (w_out, a["out_proj_w"].rearrange("(t p) o -> p t o", p=128)),
             (lncol[:, 0, :], columns(a["ln1_w"], P)), (lncol[:, 1, :], columns(a["ln1_b"], P)),
             (cw[:, 0:3, :], cwd[0:D2, :].rearrange("(t p) k -> p t k", p=128)),
             (cw[0:DS, 3, :], cwd[D2:D2 + DS, :]), (cw[0:DS, 4, :], cwd[D2 + DS:, :]),
             (cb[:, 0:3], columns(a["conv1d_b"][0:D2], 128)), (cb[0:DS, 3:4], cbd[D2:D2 + DS, :]),
             (cb[0:DS, 4:5], cbd[D2 + DS:, :]), (rms, columns(a["rms_w"], 128)),
             (dt_bias, a["dt_bias"].partition_broadcast(128)), (neg_a, a["A_log"].partition_broadcast(128)),
             (skip, a["D_skip"].partition_broadcast(128))]
    load_all(nc, loads, None)
    with Stage(nc, "filled", "negated") as (filled, negated), nc.Block() as block:
        @block.scalar
        def _(act):
            nc.scalar.activation(neg_a, neg_a, ACT.Exp).then_inc(negated, 1)
            act.wait_ge(negated, 1)
            nc.scalar.mul(neg_a, neg_a, -1.0)
            for t in range(N2):
                nc.scalar.activation(w_out[:, t, :], w_out[:, t, :], ACT.Copy, scale=rms[:, t:t + 1])

        @block.gpsimd
        def _(pool):
            nc.gpsimd.memset(upto, 1.0).then_inc(filled, 1)
            nc.gpsimd.memset(after, 1.0).then_inc(filled, 1)
            nc.gpsimd.memset(ones, 1.0)
            nc.gpsimd.memset(state, 0.0)
            nc.gpsimd.memset(m.hist[:, :, :], 0.0)
            pool.wait_ge(filled, 2)
            nc.gpsimd.affine_select(out=upto, in_=upto, compare_op=ALU.is_ge, fill=0.0, base=0,
                                    pattern=[[1, Q]], channel_multiplier=-1)
            nc.gpsimd.affine_select(out=after, in_=after, compare_op=ALU.is_gt, fill=0.0, base=0,
                                    pattern=[[-1, Q]], channel_multiplier=1)

    def heads(v, n=HD):
        return v.rearrange("p (h o) -> p h o", o=1).broadcast_to([v.shape[0], HEADS, n])

    def by_head(v):
        return v.rearrange("p (h d) -> p h d", h=HEADS)

    parts_of = (128, 128, 128, DS, DS)
    offs = (0, 128, 256, D2, D2 + DS)
    names = ("taken", "ones_set", "zdt_mm", "xbc_mm", "history", "xbc_in", "conv_tap", "conv_out", "gated", "dt_in", "dt_step",
             "dt_done", "da_done", "sums_mm", "decays", "tok_mm", "tok_out", "xdt_done", "xdl_done", "r_done", "seg_mm",
             "e_done", "cb_mm", "cbm_done", "scored_done", "y_mm", "y_read", "inter_mm", "state_mm", "state_done",
             "y_step", "y_gated", "y_squared", "rms_log", "rms_rstd", "y_normed", "yt_mm", "yt_out", "out_mm",
             "skipped") + LayerNorm.NAMES
    with nc.Fori(0, NT) as s:
        with Stage(nc, *names) as sems, nc.Block() as block:
            at = dict(zip(names, sems))

            @block.scalar
            def _(act):
                nc.scalar.copy(xin, xs[:, :, bass.ds(s * T, T)]).then_inc(at["taken"], 1)
                ln.act(act, at, h)
                act.wait_ge(at["dt_in"], 1)
                nc.scalar.activation(dte, dtr, ACT.Abs).then_inc(at["dt_step"], 1)
                act.wait_ge(at["dt_step"], 1)
                nc.scalar.activation(dte, dte, ACT.Exp, scale=-1.0).then_inc(at["dt_step"], 1)
                act.wait_ge(at["dt_step"], 2)
                nc.scalar.activation(dtw, dte, ACT.Identity, bias=1.0).then_inc(at["dt_step"], 1)
                act.wait_ge(at["dt_step"], 3)
                nc.scalar.activation(dtl, dtw, ACT.Ln).then_inc(at["dt_step"], 1)
                nc.scalar.copy(xb[:, :, 0:3], m.hist[:, :, :]).then_inc(at["history"], 1)
                for i, n in enumerate(parts_of):
                    act.wait_ge(at["xbc_mm"], i + 1)
                    nc.scalar.copy(xb[0:n, i, 3:], m.ps[0:n, 2 + i % 2, :]).then_inc(at["xbc_in"], 1)
                act.wait_ge(at["sums_mm"], 1)
                nc.scalar.activation(dec, m.ps[:, 1, 0:3 * NQ * HEADS].rearrange("p (a q h) -> p a q h", a=3, q=NQ),
                                     ACT.Exp).then_inc(at["decays"], 1)
                for i, n in enumerate(parts_of):
                    act.wait_ge(at["conv_tap"], 4 * (i + 1))
                    nc.scalar.activation(xbc[0:n, i, :], xbc[0:n, i, :], ACT.Silu, bias=cb[0:n, i:i + 1]).then_inc(at["conv_out"], 1)
                for q in range(NQ):
                    nc.scalar.activation(sz[:, q, :], m.ps[:, 4 + q, 0:D2], ACT.Silu).then_inc(at["gated"], 1)
                for q in range(NQ):
                    act.wait_ge(at["tok_mm"], q + 1)
                    nc.scalar.copy(xtok[:, q, :], m.ps[:, q % 2, 0:D2 + DS]).then_inc(at["tok_out"], 1)
                for q in range(NQ):
                    act.wait_ge(at["seg_mm"], q + 1)
                    if q >= 2:
                        act.wait_ge(at["scored_done"], q - 1)
                    nc.scalar.activation(e[:, q % 2, :].rearrange("p (a b) -> p a b", b=HEADS * Q // 2),
                                         m.ps[:, 2:4, 0:HEADS * Q // 2], ACT.Exp).then_inc(at["e_done"], 1)
                for q in range(NQ):
                    act.wait_ge(at["y_gated"], q + 1)
                    nc.scalar.activation(xdl[:, q, :], y[:, q, :], ACT.Square, accum_out=ss[:, q:q + 1]).then_inc(at["y_squared"], 1)
                act.wait_ge(at["y_squared"], NQ)
                nc.scalar.activation(ss, ss, ACT.Ln, scale=1.0 / D2, bias=m.eps[:, :]).then_inc(at["rms_log"], 1)
                act.wait_ge(at["rms_log"], 1)
                nc.scalar.activation(ss, ss, ACT.Exp, scale=-0.5).then_inc(at["rms_rstd"], 1)
                act.wait_ge(at["rms_rstd"], 1)
                for q in range(NQ):
                    nc.scalar.activation(y[:, q, :], y[:, q, :], ACT.Copy, scale=ss[:, q:q + 1]).then_inc(at["y_normed"], 1)
                for t in range(N2):
                    act.wait_ge(at["yt_mm"], t + 1)
                    nc.scalar.copy(yt[:, t, :], m.ps[:, t, :]).then_inc(at["yt_out"], 1)

            @block.tensor
            def _(pe):
                pe.wait_ge(at["taken"], 1)
                pe.wait_ge(at["ones_set"], 1)
                ln.pe(pe, at, xin)
                pe.wait_ge(at["ln_out"], NH)
                for q in range(NQ):
                    for t in range(NH):
                        ins = nc.tensor.matmul(m.ps[:, 4 + q, 0:DIN0], h[:, t, q * Q:(q + 1) * Q], w_zdt[:, t, :],
                                               start=(t == 0), stop=(t == NH - 1))
                    ins.then_inc(at["zdt_mm"], 1)
                for i, n in enumerate(parts_of):
                    if i >= 2:
                        pe.wait_ge(at["xbc_in"], i - 1)
                    for t in range(NH):
                        ins = nc.tensor.matmul(m.ps[0:n, 2 + i % 2, :], w_xbc[:, t, offs[i]:offs[i] + n], h[:, t, :],
                                               start=(t == 0), stop=(t == NH - 1))
                    ins.then_inc(at["xbc_mm"], 1)
                pe.wait_ge(at["da_done"], 1)
                for i, lhs in enumerate((upto, after, ones)):
                    ins = nc.tensor.matmul(m.ps[:, 1, i * NQ * HEADS:(i + 1) * NQ * HEADS], lhs,
                                           da.rearrange("p q h -> p (q h)"), start=True, stop=True)
                ins.then_inc(at["sums_mm"], 1)
                pe.wait_ge(at["decays"], 1)
                pe.wait_ge(at["conv_out"], 5)
                for q in range(NQ):
                    if q >= 2:
                        pe.wait_ge(at["tok_out"], q - 1)
                    for i, n in enumerate(parts_of[:4]):
                        ins = nc.tensor.transpose(m.ps[:, q % 2, offs[i]:offs[i] + n], xbc[0:n, i, q * Q:(q + 1) * Q],
                                                  m.ident[0:n, 0:n])
                    ins.then_inc(at["tok_mm"], 1)
                pe.wait_ge(at["tok_out"], NQ)
                pe.wait_ge(at["gated"], NQ)
                for q in range(NQ):
                    tok = slice(q * Q, (q + 1) * Q)
                    if q >= 1:
                        pe.wait_ge(at["e_done"], q)
                    pe.wait_ge(at["r_done"], q + 1)
                    for i in range(2):
                        ins = nc.tensor.matmul(m.ps[:, 2 + i, 0:HEADS * Q // 2], after,
                                               r[:, q % 2, i * HEADS * Q // 2:(i + 1) * HEADS * Q // 2], start=True, stop=True)
                    ins.then_inc(at["seg_mm"], 1)
                    if q >= 1:
                        pe.wait_ge(at["cbm_done"], q)
                    nc.tensor.matmul(m.ps[:, 0, 0:Q], xbc[0:DS, 3, tok], xbc[0:DS, 4, tok], start=True, stop=True).then_inc(at["cb_mm"], 1)
                    pe.wait_ge(at["xdl_done"], q + 1)
                    if q >= 1:
                        pe.wait_ge(at["state_done"], q)
                    nc.tensor.matmul(m.ps[:, 5, 0:D2], xbc[0:DS, 4, tok], state, start=True, stop=True).then_inc(at["inter_mm"], 1)
                    nc.tensor.matmul(m.ps[0:DS, 6, 0:D2], xtok[:, q, D2:D2 + DS], xdl[:, q, :], start=True, stop=True).then_inc(at["state_mm"], 1)
                    pe.wait_ge(at["scored_done"], q + 1)
                    if q >= 1:
                        pe.wait_ge(at["y_read"], q)
                    for hd in range(HEADS):
                        ins = nc.tensor.matmul(m.ps[:, 4, hd * HD:(hd + 1) * HD], e[:, q % 2, hd * Q:(hd + 1) * Q],
                                               xdt[:, q, hd * HD:(hd + 1) * HD], start=True, stop=True)
                    ins.then_inc(at["y_mm"], 1)
                pe.wait_ge(at["y_normed"], NQ)
                for t in range(N2):
                    for q in range(NQ):
                        ins = nc.tensor.transpose(m.ps[:, t, q * Q:(q + 1) * Q], y[:, q, t * 128:(t + 1) * 128], m.ident[:, :])
                    ins.then_inc(at["yt_mm"], 1)
                for c in range(NH):
                    for t in range(N2):
                        pe.wait_ge(at["yt_out"], t + 1)
                        ins = nc.tensor.matmul(m.ps[0:P, 6 + c, :], w_out[:, t, c * P:(c + 1) * P], yt[:, t, :],
                                               start=(t == 0), stop=(t == N2 - 1))
                    ins.then_inc(at["out_mm"], 1)

            @block.vector
            def _(dve):
                ln.constants().then_inc(at["ones_set"], 1)
                dve.wait_ge(at["taken"], 1)
                ln.dve(dve, at, xin)
                for q in range(NQ):
                    dve.wait_ge(at["zdt_mm"], q + 1)
                    ins = nc.vector.tensor_tensor(dtr[:, q * HEADS:(q + 1) * HEADS], m.ps[:, 4 + q, D2:DIN0], dt_bias, ALU.add)
                ins.then_inc(at["dt_in"], 1)
                dve.wait_ge(at["dt_step"], 4)
                nc.vector.scalar_tensor_tensor(dtw, dtw, 1.0, dte, ALU.subtract, ALU.subtract).then_inc(at["dt_done"], 1)
                dve.wait_ge(at["dt_done"], 1)
                nc.vector.tensor_tensor(dtl, dtl, dtw, ALU.subtract).then_inc(at["dt_done"], 1)
                dve.wait_ge(at["dt_done"], 2)
                nc.vector.scalar_tensor_tensor(dt, dtr, 0.0, dtl, ALU.max, ALU.add).then_inc(at["dt_done"], 1)
                dve.wait_ge(at["dt_done"], 3)
                nc.vector.tensor_tensor(da, dt.rearrange("p (q h) -> p q h", q=NQ),
                                        neg_a.rearrange("p (o h) -> p o h", o=1).broadcast_to([128, NQ, HEADS]), ALU.mult).then_inc(at["da_done"], 1)
                dve.wait_ge(at["history"], 1)
                for i, n in enumerate(parts_of):
                    dve.wait_ge(at["xbc_in"], i + 1)
                    nc.vector.tensor_scalar(xbc[0:n, i, :], xb[0:n, i, 0:T], cw[0:n, i, 0:1], None, ALU.mult).then_inc(at["conv_tap"], 1)
                    for k in range(1, 4):
                        dve.wait_ge(at["conv_tap"], 4 * i + k)
                        nc.vector.scalar_tensor_tensor(xbc[0:n, i, :], xb[0:n, i, k:k + T], cw[0:n, i, k:k + 1], xbc[0:n, i, :],
                                                       ALU.mult, ALU.add).then_inc(at["conv_tap"], 1)
                    nc.vector.tensor_copy(m.hist[0:n, i, :], xb[0:n, i, T:T + 3])
                for q in range(NQ):
                    dve.wait_ge(at["tok_out"], q + 1)
                    nc.vector.tensor_tensor(by_head(xdt[:, q, :]), by_head(xtok[:, q, 0:D2]),
                                            heads(dt[:, q * HEADS:(q + 1) * HEADS]), ALU.mult).then_inc(at["xdt_done"], 1)
                    dve.wait_ge(at["xdt_done"], q + 1)
                    nc.vector.tensor_tensor(by_head(xdl[:, q, :]), by_head(xdt[:, q, :]), heads(dec[:, 1, q, :]), ALU.mult).then_inc(at["xdl_done"], 1)
                for q in range(NQ):
                    dve.wait_ge(at["cb_mm"], q + 1)
                    nc.vector.tensor_tensor(cbm[:, q % 2, :], m.ps[:, 0, 0:Q], upto, ALU.mult).then_inc(at["cbm_done"], 1)
                    dve.wait_ge(at["cbm_done"], q + 1)
                    dve.wait_ge(at["e_done"], q + 1)
                    e3 = e[:, q % 2, :].rearrange("p (h i) -> p h i", h=HEADS)
                    nc.vector.tensor_tensor(e3, e3, cbm[:, q % 2, :].rearrange("p (o i) -> p o i", o=1).broadcast_to([128, HEADS, Q]),
                                            ALU.mult).then_inc(at["scored_done"], 1)
                    dve.wait_ge(at["inter_mm"], q + 1)
                    nc.vector.tensor_tensor(by_head(state), by_head(state), heads(dec[0:DS, 2, q, :]), ALU.mult).then_inc(at["y_step"], 1)
                    yq = y[:, q, :]
                    nc.vector.tensor_tensor(by_head(yq), by_head(m.ps[:, 5, 0:D2]), heads(dec[:, 0, q, :]), ALU.mult).then_inc(at["y_step"], 1)
                    dve.wait_ge(at["state_mm"], q + 1)
                    dve.wait_ge(at["y_step"], 3 * q + 1)
                    nc.vector.tensor_tensor(state, state, m.ps[0:DS, 6, 0:D2], ALU.add).then_inc(at["state_done"], 1)
                    dve.wait_ge(at["y_mm"], q + 1)
                    dve.wait_ge(at["y_step"], 3 * q + 2)
                    nc.vector.tensor_tensor(yq, yq, m.ps[:, 4, 0:D2], ALU.add).then_inc(at["y_read"], 1)
                    dve.wait_ge(at["y_read"], q + 1)
                    dve.wait_ge(at["skipped"], q + 1)
                    nc.vector.tensor_tensor(yq, yq, xtok[:, q, 0:D2], ALU.add).then_inc(at["y_step"], 1)
                    dve.wait_ge(at["y_step"], 3 * q + 3)
                    nc.vector.tensor_tensor(yq, yq, sz[:, q, :], ALU.mult).then_inc(at["y_gated"], 1)
                for c in range(NH):
                    dve.wait_ge(at["out_mm"], c + 1)
                    blk = xs[:, c:c + 1, bass.ds(s * T, T)].rearrange("p a t -> p (a t)")
                    nc.vector.tensor_tensor(blk, xin[:, c, :], m.ps[0:P, 6 + c, :], ALU.add)

            @block.gpsimd
            def _(pool):
                pool.wait_ge(at["da_done"], 1)
                for q in range(NQ):
                    if q >= 2:
                        pool.wait_ge(at["seg_mm"], q - 1)
                    nc.gpsimd.tensor_tensor(r[:, q % 2, :].rearrange("p (h i) -> p h i", h=HEADS),
                                            upto.rearrange("p (o i) -> p o i", o=1).broadcast_to([128, HEADS, Q]),
                                            heads(da[:, q, :], Q), ALU.mult).then_inc(at["r_done"], 1)
                for q in range(NQ):
                    pool.wait_ge(at["xdt_done"], q + 1)
                    nc.gpsimd.tensor_tensor(by_head(xtok[:, q, 0:D2]), by_head(xtok[:, q, 0:D2]), heads(skip), ALU.mult).then_inc(at["skipped"], 1)


def project(m, xn, xa, w_in):
    nc = m.nc
    m.start(7)
    w = m.take(NH, D2, parts=P)
    load_all(nc, [(w, w_in.rearrange("(t p) o -> p t o", p=P)[:, :, 0:D2])], None)
    with Stage(nc, "proj_mm", "act_taken", "dve_taken") as (proj_mm, act_taken, dve_taken), nc.Block() as block:
        steps = [(i, c) for i in range(NT) for c in range(N2)]

        @block.tensor
        def _(pe):
            for n, (i, c) in enumerate(steps):
                if n >= 8:
                    pe.wait_ge(dve_taken if n % 2 else act_taken, n // 2 - 3)
                for t in range(NH):
                    ins = nc.tensor.matmul(m.ps[:, n % 8, :], w[:, t, c * 128:(c + 1) * 128], xn[:, t, i * T:(i + 1) * T],
                                           start=(t == 0), stop=(t == NH - 1))
                ins.then_inc(proj_mm, 1)

        @block.scalar
        def _(act):
            for n, (i, c) in enumerate(steps):
                if n % 2 == 0:
                    act.wait_ge(proj_mm, n + 1)
                    nc.scalar.copy(xa[:, c, i * T:(i + 1) * T], m.ps[:, n % 8, :]).then_inc(act_taken, 1)

        @block.vector
        def _(dve):
            for n, (i, c) in enumerate(steps):
                if n % 2:
                    dve.wait_ge(proj_mm, n + 1)
                    nc.vector.tensor_copy(xa[:, c, i * T:(i + 1) * T], m.ps[:, n % 8, :]).then_inc(dve_taken, 1)


def selective_scan(m, xc, y, a):
    nc = m.nc
    m.start(0)
    bbc = m.take(NS, T)
    delta = m.take(2, N2, T)
    du = m.take(2, N2, T)
    hs = m.take(3, T)
    hc = m.take(2, T)
    dbu = m.take(4, T)
    xd = m.take(T)
    rest = m.take(T)
    mid, low = (m.take(T // 2).bitcast(BF16) for _ in range(2))
    sp_e, sp_w, sp_l = m.take(T), m.take(T), m.take(T)
    parts = m.take(T).bitcast(BF16).rearrange("p (a b) -> p a b", a=2)
    xpw = m.take(K4, N2, P + DTR)
    assert m.top <= 6 * SLOT
    m.start(SLOTS)
    dtw = m.take(K4, D2)
    aneg = m.take(K4, N2, NS)
    dtb = m.take(K4, N2)
    dsk = m.take(K4, N2)
    carry = m.take(N2, NS)
    BC = 2 * NS
    xw = a["x_proj_w"]
    loads = []
    for k in range(K4):
        src = xw[:, k, :].rearrange("(t p) c -> p t c", p=128)
        for i in range(3):
            loads.append((xpw[:, k, :, BC * i:BC * (i + 1)], src[:, :, DTR:]))
        loads.append((xpw[:, k, :, P:], src[:, :, 0:DTR]))
        loads.append((dtw[P:P + DTR, k, :], a["dt_w"][:, k, :]))
        loads.append((aneg[:, k, :, :], a["A_logs"][k * D2:(k + 1) * D2, :].rearrange("(t p) n -> p t n", p=128)))
        loads.append((dtb[:, k, :], columns(a["dt_b"][k, :], 128)))
        loads.append((dsk[:, k, :], columns(a["Ds"][k * D2:(k + 1) * D2], 128)))
    load_all(nc, loads, None)
    with Stage(nc, "exped", "summed") as (exped, summed), nc.Block() as block:
        @block.scalar
        def _(act):
            nc.scalar.activation(aneg, aneg, ACT.Exp).then_inc(exped, 1)
            act.wait_ge(exped, 1)
            nc.scalar.mul(aneg, aneg, -1.0)

        @block.vector
        def _(dve):
            for k in range(1, K4):
                nc.vector.tensor_tensor(dsk[:, 0, :], dsk[:, 0, :], dsk[:, k, :], ALU.add).then_inc(summed, 1)
                dve.wait_ge(summed, k)
            for t in range(N2):
                nc.vector.tensor_scalar(y[:, t, :], xc[:, t, :], dsk[:, 0, t:t + 1], None, ALU.mult)

    def block_of(k, v, t, i):
        i = (NT - 1 - i) if k >= 2 else i
        if k % 2 == 0:
            return v[:, t:t + 1, bass.ds(i * T, T)].rearrange("p a t -> p (a t)")
        wide = T // H
        return v.rearrange("p t (h w) -> p t w h", w=W)[:, t:t + 1, bass.ds(i * wide, wide), :].rearrange("p a w h -> p (a w) h")

    def shaped(k, v):
        return v if k % 2 == 0 else v.rearrange("p (w h) -> p w h", h=H)

    names = ("xd_mm", "hi_out", "xd_out", "split", "parts_out", "dl_mm", "sp_act", "sp_pool", "bb_mm", "bb_out",
             "da_ready", "db_ready", "scanned", "saved", "c_mm", "hc_ready", "y_mm", "y_added")

    def pe_ahead(pe, at, k, w, i, par, o):
        if w == 1:
            if o:
                pe.wait_ge(at["sp_act"], 6 * N2 * o)
            for t in range(N2):
                ins = nc.tensor.matmul(shaped(k, m.ps[0:P + DTR, 7, :]), xpw[:, k, t, :], block_of(k, xc, t, i),
                                       start=(t == 0), stop=(t == N2 - 1))
            ins.then_inc(at["xd_mm"], 1)
        if w in (7, 15, 23):
            t = (w - 7) // 8
            pe.wait_ge(at["xd_out"], o + 1)
            if t:
                pe.wait_ge(at["sp_act"], 6 * (N2 * o + t - 1) + 2)
            nc.tensor.matmul(m.ps[:, 7, :], dtw[P:P + DTR, k, t * 128:(t + 1) * 128], xd[P:P + DTR, :],
                             start=True, stop=True, tile_position=(P, 0)).then_inc(at["dl_mm"], 1)
        if 32 <= w < 48:
            n = w - 32
            if w == 32:
                pe.wait_ge(at["parts_out"], 2 * (o + 1))
            if NS * o + n:
                pe.wait_ge(at["bb_out"], NS * o + n)
            nc.tensor.matmul(m.ps[:, 6, :], m.sel[:, n:n + 1].broadcast_to([P, 128]), parts[0:P, par, :],
                             start=True, stop=True).then_inc(at["bb_mm"], 1)

    def act_ahead(act, at, k, w, i, par, o, units=None):
        if w == 3:
            act.wait_ge(at["xd_mm"], o + 1)
            nc.scalar.copy(parts[0:P, par, :], m.ps[0:P, 7, :]).then_inc(at["hi_out"], 1)
        if w == 4:
            if o:
                act.wait_ge(at["split"], 3 * o)
                act.wait_ge(at["dl_mm"], N2 * o)
            nc.scalar.copy(xd[0:P + DTR, :], m.ps[0:P + DTR, 7, :]).then_inc(at["xd_out"], 1)
        if w == 14:
            act.wait_ge(at["split"], 3 * (o + 1))
            nc.scalar.copy(parts[32:64, par, :], mid[32:64, :]).then_inc(at["parts_out"], 1)
        if w == 15:
            nc.scalar.copy(parts[64:96, par, :], low[64:96, :]).then_inc(at["parts_out"], 1)
        if 8 <= w < 32 and w % 8 < 6:
            t, j = w // 8 - 1, w % 8
            done = 6 * (N2 * o + t) + j
            bias = dtb[:, k, t:t + 1]
            if j == 0:
                act.wait_ge(at["dl_mm"], N2 * o + t + 1)
                if N2 * o + t:
                    act.wait_ge(at["sp_pool"], 4 * (N2 * o + t))
                ins = nc.scalar.activation(sp_e, m.ps[:, 7, :], ACT.Abs, bias=bias)
            elif j == 1:
                ins = nc.scalar.activation(delta[:, par, t, :], m.ps[:, 7, :], ACT.Relu, bias=bias)
            elif j == 2:
                act.wait_ge(at["sp_act"], done - 1)
                ins = nc.scalar.activation(sp_e, sp_e, ACT.Exp, scale=-1.0)
            elif j == 3:
                act.wait_ge(at["sp_act"], done)
                ins = nc.scalar.activation(sp_w, sp_e, ACT.Identity, bias=1.0)
            elif j == 4:
                act.wait_ge(at["sp_act"], done)
                ins = nc.scalar.activation(sp_l, sp_w, ACT.Ln)
            else:
                act.wait_ge(at["sp_act"], done)
                ins = nc.scalar.activation(sp_w, sp_w, ACT.Identity, bias=minus_one)
            ins.then_inc(at["sp_act"], 1)
        if 33 <= w < 49:
            n = w - 33
            act.wait_ge(at["bb_mm"], NS * o + n + 1)
            if units is not None:
                act.wait_ge(at["db_ready"], units + 33 + n)
            nc.scalar.copy(bbc[:, n, :], m.ps[:, 6, :]).then_inc(at["bb_out"], 1)

    def pool_ahead(pool, at, k, w, i, par, o):
        if w == 5:
            pool.wait_ge(at["xd_out"], o + 1)
            nc.gpsimd.tensor_tensor(rest[0:P, :], xd[0:P, :], parts[0:P, par, :], ALU.subtract).then_inc(at["split"], 1)
        if w == 6:
            pool.wait_ge(at["split"], 3 * o + 1)
            if o:
                pool.wait_ge(at["parts_out"], 2 * o)
            nc.gpsimd.tensor_copy(mid[0:P, :], rest[0:P, :]).then_inc(at["split"], 1)
        if w == 7:
            pool.wait_ge(at["split"], 3 * o + 2)
            nc.gpsimd.tensor_tensor(low[0:P, :], rest[0:P, :], mid[0:P, :], ALU.subtract).then_inc(at["split"], 1)
        if 14 <= w < 34 and (w - 14) % 8 < 4:
            t, j = (w - 14) // 8, (w - 14) % 8
            done = 4 * (N2 * o + t) + j
            if j == 0:
                pool.wait_ge(at["sp_act"], 6 * (N2 * o + t + 1))
                ins = nc.gpsimd.tensor_tensor(sp_w, sp_w, sp_e, ALU.subtract)
            else:
                pool.wait_ge(at["sp_pool"], done)
                if j == 1:
                    ins = nc.gpsimd.tensor_tensor(sp_l, sp_l, sp_w, ALU.subtract)
                elif j == 2:
                    ins = nc.gpsimd.tensor_tensor(delta[:, par, t, :], delta[:, par, t, :], sp_l, ALU.add)
                else:
                    ins = nc.gpsimd.tensor_tensor(shaped(k, du[:, par, t, :]), shaped(k, delta[:, par, t, :]),
                                                  block_of(k, xc, t, i), ALU.mult)
            ins.then_inc(at["sp_pool"], 1)

    minus_one = m.take(1)
    for k in range(K4):
        back = k >= 2
        flip = (lambda v: v[:, ::-1]) if back else (lambda v: v)
        last = 0 if back else T - 1
        with Stage(nc, *names) as sems, nc.Block() as block:
            at = dict(zip(names, sems))

            @block.vector
            def _(dve):
                nc.vector.memset(carry, 0.0)
                nc.vector.memset(minus_one, -1.0).then_inc(at["scanned"], 1)

            @block.tensor
            def _(pe):
                for w in range(49):
                    pe_ahead(pe, at, k, w, 0, 0, 0)

            @block.scalar
            def _(act):
                act.wait_ge(at["scanned"], 1)
                for w in range(49):
                    act_ahead(act, at, k, w, 0, 0, 0)

            @block.gpsimd
            def _(pool):
                for w in range(49):
                    pool_ahead(pool, at, k, w, 0, 0, 0)

        with nc.Fori(0, NT // 2) as pair:
            with Stage(nc, *names) as sems, nc.Block() as block:
                at = dict(zip(names, sems))
                ALL = 2 * UNITS

                def unit(v):
                    return v // UNITS, v % UNITS // NS, v % NS

                def after(par):
                    return (2 * pair + par + 1) % NT

                @block.tensor
                def _(pe):
                    def add_up(v):
                        par, t, n = unit(v)
                        g = v // NS
                        pe.wait_ge(at["hc_ready"], v + 1)
                        if n == 0 and g >= 2:
                            pe.wait_ge(at["y_added"], g - 1)
                        nc.tensor.matmul(m.ps[:, g % 2, :], m.ident[:, :], hc[:, v % 2, :],
                                         start=(n == 0), stop=(n == NS - 1)).then_inc(at["y_mm"], 1)

                    for v in range(ALL):
                        par, t, n = unit(v)
                        if v >= 2:
                            pe.wait_ge(at["hc_ready"], v - 1)
                        if v == UNITS:
                            pe.wait_ge(at["parts_out"], 2)
                        nc.tensor.matmul(m.ps[:, 4 + v % 2, :], m.sel[:, NS + n:NS + n + 1].broadcast_to([P, 128]),
                                         parts[0:P, par, :], start=True, stop=True).then_inc(at["c_mm"], 1)
                        if v:
                            add_up(v - 1)
                        pe_ahead(pe, at, k, v % UNITS, after(par), 1 - par, par)
                    add_up(ALL - 1)

                @block.scalar
                def _(act):
                    def save(v):
                        par, t, n = unit(v)
                        act.wait_ge(at["scanned"], v + 1)
                        nc.scalar.copy(carry[:, t, n:n + 1], hs[:, v % 3, last:last + 1]).then_inc(at["saved"], 1)

                    for v in range(ALL):
                        par, t, n = unit(v)
                        if v >= 2:
                            act.wait_ge(at["scanned"], v - 1)
                        if v >= UNITS and n == 0:
                            act.wait_ge(at["sp_pool"], 4 * (t + 1))
                        nc.scalar.activation(m.ps[:, 2 + v % 2, :], delta[:, par, t, :], ACT.Exp,
                                             scale=aneg[:, k, t, n:n + 1]).then_inc(at["da_ready"], 1)
                        if v >= 2:
                            save(v - 2)
                        if v == UNITS:
                            act_ahead(act, at, k, UNITS, None, 1, 0, 0)
                        act_ahead(act, at, k, v % UNITS, after(par), 1 - par, par, par * UNITS)
                    save(ALL - 2)
                    save(ALL - 1)
                    act_ahead(act, at, k, UNITS, None, 0, 1, UNITS)

                @block.gpsimd
                def _(pool):
                    for v in range(ALL):
                        par, t, n = unit(v)
                        if v >= 4:
                            pool.wait_ge(at["scanned"], v - 3)
                        if v >= UNITS and t == 0:
                            pool.wait_ge(at["bb_out"], n + 1)
                            if n == 0:
                                pool.wait_ge(at["sp_pool"], 4 * N2)
                        nc.gpsimd.tensor_tensor(dbu[:, v % 4, :], du[:, par, t, :], bbc[:, n, :], ALU.mult).then_inc(at["db_ready"], 1)
                        pool_ahead(pool, at, k, v % UNITS, after(par), 1 - par, par)

                @block.vector
                def _(dve):
                    def times_c(v):
                        dve.wait_ge(at["scanned"], v + 1)
                        dve.wait_ge(at["c_mm"], v + 1)
                        if v >= 2:
                            dve.wait_ge(at["y_mm"], v - 1)
                        nc.vector.tensor_tensor(hc[:, v % 2, :], hs[:, v % 3, :], m.ps[:, 4 + v % 2, :],
                                                ALU.mult).then_inc(at["hc_ready"], 1)

                    def take_y(g):
                        par, t, n = unit(g * NS)
                        dve.wait_ge(at["y_mm"], NS * (g + 1))
                        out = block_of(k, y, t, 2 * pair + par)
                        nc.vector.tensor_tensor(out, out, shaped(k, m.ps[:, g % 2, :]), ALU.add).then_inc(at["y_added"], 1)

                    for v in range(ALL):
                        par, t, n = unit(v)
                        dve.wait_ge(at["da_ready"], v + 1)
                        dve.wait_ge(at["db_ready"], v + 1)
                        if v >= 3:
                            dve.wait_ge(at["saved"], v - 2)
                            dve.wait_ge(at["hc_ready"], v - 2)
                        if v >= UNITS:
                            dve.wait_ge(at["saved"], v - UNITS + 1)
                        nc.vector.tensor_tensor_scan(flip(hs[:, v % 3, :]), flip(m.ps[:, 2 + v % 2, :]), flip(dbu[:, v % 4, :]),
                                                     carry[:, t, n:n + 1], ALU.mult, ALU.add).then_inc(at["scanned"], 1)
                        if v:
                            times_c(v - 1)
                        if v >= NS and n == 3:
                            take_y(v // NS - 1)
                    times_c(ALL - 1)
                    take_y(ALL // NS - 1)


def finish_scan(m, y, x, x1, a):
    nc = m.nc
    m.start(2)
    wz = m.take(NH, D2, parts=P)
    wo = m.take(N2, C)
    cols = m.take(2, N2)
    ln = LayerNorm(m, N2, 128, cols[:, 0, :], cols[:, 1, :])
    xn = m.take(NH, T, parts=P)
    yin = m.take(N2, T)
    sz = m.take(N2, T)
    h = m.take(N2, T)
    g = m.take(N2, T)
    load_all(nc, [(x[:, t, :], x1[:, t, :]) for t in range(NH)] +
             [(wz, a["in_proj_w"].rearrange("(t p) o -> p t o", p=P)[:, :, D2:]),
              (wo, a["out_proj_w"].rearrange("(t p) o -> p t o", p=128)),
              (cols[:, 0, :], columns(a["out_norm_w"], 128)), (cols[:, 1, :], columns(a["out_norm_b"], 128))], None)
    names = ("taken", "ones_set", "xn_done", "z_mm", "z_out", "gated", "out_mm") + LayerNorm.NAMES
    with nc.Fori(0, NT) as s:
        with Stage(nc, *names) as sems, nc.Block() as block:
            at = dict(zip(names, sems))

            @block.scalar
            def _(act):
                nc.scalar.copy(yin, y[:, :, bass.ds(s * T, T)]).then_inc(at["taken"], 1)
                ln.act(act, at, h)
                for o in range(N2):
                    act.wait_ge(at["z_mm"], o + 1)
                    nc.scalar.activation(sz[:, o, :], m.ps[:, 2 + o, :], ACT.Silu).then_inc(at["z_out"], 1)

            @block.tensor
            def _(pe):
                pe.wait_ge(at["taken"], 1)
                pe.wait_ge(at["ones_set"], 1)
                ln.pe(pe, at, yin)
                pe.wait_ge(at["xn_done"], 1)
                for o in range(N2):
                    for t in range(NH):
                        ins = nc.tensor.matmul(m.ps[:, 2 + o, :], wz[:, t, o * 128:(o + 1) * 128], xn[:, t, :],
                                               start=(t == 0), stop=(t == NH - 1))
                    ins.then_inc(at["z_mm"], 1)
                for c in range(NH):
                    for t in range(N2):
                        pe.wait_ge(at["gated"], t + 1)
                        ins = nc.tensor.matmul(m.ps[0:P, 6 + c, :], wo[:, t, c * P:(c + 1) * P], g[:, t, :],
                                               start=(t == 0), stop=(t == N2 - 1))
                    ins.then_inc(at["out_mm"], 1)

            @block.vector
            def _(dve):
                ln.constants().then_inc(at["ones_set"], 1)
                for t in range(NH):
                    ins = nc.vector.tensor_scalar(xn[:, t, :], x[:, t:t + 1, bass.ds(s * T, T)].rearrange("p a t -> p (a t)"),
                                                  m.gn_mean[:, t:t + 1], m.gn_rstd[:, t:t + 1], ALU.subtract, ALU.mult)
                ins.then_inc(at["xn_done"], 1)
                dve.wait_ge(at["taken"], 1)
                ln.dve(dve, at, yin)
                for t in range(N2):
                    dve.wait_ge(at["ln_out"], t + 1)
                    dve.wait_ge(at["z_out"], t + 1)
                    nc.vector.tensor_tensor(g[:, t, :], h[:, t, :], sz[:, t, :], ALU.mult).then_inc(at["gated"], 1)
                for c in range(NH):
                    dve.wait_ge(at["out_mm"], c + 1)
                    blk = x[:, c:c + 1, bass.ds(s * T, T)].rearrange("p a t -> p (a t)")
                    nc.vector.tensor_tensor(blk, blk, m.ps[0:P, 6 + c, :], ALU.add)


def store(nc, dst, src):
    with Stage(nc, "stored") as (stored,), nc.Block() as block:
        @block.sync
        def _(sp):
            for t in range(src.shape[1]):
                sp.dma_start(dst[:, t, :], src[:, t, :]).then_inc(stored, 16)
            sp.wait_ge(stored, 16 * src.shape[1])


def layers(nc, x, out, x1, l0, l1, l2, l3, samples=B, debug=None):
    with ExitStack() as ctx:
        m = Chip(nc, ctx)
        constants(m)
        x1v = x1.rearrange("(t p) l -> p t l", p=P)
        with nc.Fori(0, samples) as b:
            xb = x[bass.ds(b, 1)].rearrange("a (t p) l -> p (a t) l", p=P)
            ob = out[bass.ds(b, 1)].rearrange("a (t p) l -> p (a t) l", p=P)
            s01, s23, s45 = m.slots(0, NH, P), m.slots(2, NH, P), m.slots(4, NH, P)

            def probe(name, v):
                if debug and name in debug:
                    store(nc, debug[name], v)

            group_norm(m, s01, s23, load=xb)
            probe("gn", s23)
            conv3x3(m, s23, s45, NH, P, l0["cpe1_w"], l0["cpe1_b"], own=True)
            probe("cpe1", s45)
            ssd(m, s45, l0)
            probe("ssd", s45)
            conv3x3(m, s45, s23, NH, P, l0["cpe2_w"], l0["cpe2_b"], own=True)
            mlp(m, s23, s01, l0)
            probe("l0", s01)
            store(nc, x1v, s01)
            group_norm(m, s01, s23)
            xa, xc, y = m.slots(4, N2), m.slots(9, N2), m.slots(6, N2)
            project(m, s23, xa, l1["in_proj_w"])
            conv3x3(m, xa, xc, N2, 128, l1["conv_w"], l1["conv_b"], silu=True)
            probe("xc", xc)
            selective_scan(m, xc, y, l1)
            probe("y", y)
            finish_scan(m, y, s01, x1v, l1)
            probe("l1", s01)
            group_norm(m, s01, s23)
            conv3x3(m, s23, s45, NH, P, l2["w"], l2["b"], residual=s01)
            group_norm(m, s45, s23)
            conv3x3(m, s23, s01, NH, P, l3["w"], l3["b"], residual=s45)
            store(nc, ob, s01)


LAYER_INS = {
    "L0_conv_": ("cpe1_w", "cpe1_b", "ln1_w", "ln1_b", "in_proj_w", "conv1d_w", "conv1d_b", "dt_bias", "A_log", "D_skip",
                 "rms_w", "out_proj_w", "cpe2_w", "cpe2_b", "ln2_w", "ln2_b", "fc1_w", "fc1_b", "fc2_w", "fc2_b"),
    "L1_conv_": ("in_proj_w", "conv_w", "conv_b", "x_proj_w", "dt_w", "dt_b", "A_logs", "Ds", "out_norm_w", "out_norm_b",
                 "out_proj_w"),
    "L2_conv_": ("w", "b"),
    "L3_conv_": ("w", "b"),
}
RENAMED = {"x_proj_w": "x_proj_weight", "dt_w": "dt_projs_weight", "dt_b": "dt_projs_bias"}


def laid_out(name, v):
    import numpy as np
    v = np.asarray(v)
    if name == "x":
        v = v.transpose(0, 3, 1, 2).reshape(v.shape[0], C, L)
    elif name in ("in_proj_w", "out_proj_w", "fc1_w", "fc2_w"):
        v = v.T
    elif name in ("cpe1_w", "cpe2_w", "conv_w"):
        v = v.reshape(-1, 9)
    elif name == "w":
        v = v.reshape(9, C).T
    elif name in ("x_proj_w", "dt_w"):
        v = v.transpose(2, 0, 1)
    return np.ascontiguousarray(v)


def program(nc, arrays, samples=B, debug=()):
    def dram(name, v):
        return nc.dram_tensor(name, v.shape, mybir.dt.from_np(v.dtype), kind="ExternalInput").ap()

    x = dram("x", arrays["x"])
    params = [{n: dram(prefix + n, arrays[prefix + n]) for n in names} for prefix, names in LAYER_INS.items()]
    out = nc.dram_tensor("out", (samples, C, L), F32, kind="ExternalOutput").ap()
    x1 = nc.dram_tensor("x1", (C, L), F32, kind="Internal").ap()
    probes = {n: nc.dram_tensor("probe_" + n, (p, t, L), F32, kind="ExternalOutput").ap() for n, p, t in debug}
    layers(nc, x, out, x1, *params, samples=samples, debug=probes)


def kernel(**inputs):
    import concourse.bacc as bacc
    from concourse.bass_utils import run_bass_kernel_spmd

    nc = bacc.Bacc("TRN2", target_bir_lowering=False, num_devices=1)
    arrays = {"x": laid_out("x", inputs["x"])}
    for prefix, names in LAYER_INS.items():
        for n in names:
            arrays[prefix + n] = laid_out(n, inputs[prefix + RENAMED.get(n, n)])
    program(nc, arrays)
    r = run_bass_kernel_spmd(nc, [arrays], core_ids=[0])
    return r.results[0]["out"].reshape(B, C, H, W).transpose(0, 2, 3, 1)
```

```python
from contextlib import ExitStack

import concourse.bass as bass
from concourse import mybir

F32 = mybir.dt.float32
BF16 = mybir.dt.bfloat16
ALU = mybir.AluOpType
ACT = mybir.ActivationFunctionType

B, H, W, C = 8, 64, 64, 192
L = H * W
P = 96
NH = C // P
GROUP = 6
T = 512
NT = L // T
ROWS = 16
D2 = 2 * C
N2 = D2 // 128
HEADS, HD, DS = 6, 64, 64
Q = 128
NQ = T // Q
DTR, NS, K4 = 12, 16, 4
TAIL = 50
UNITS = N2 * NS
DIN0 = D2 + HEADS
MLP = 4 * C
NM = MLP // 128
CENTRE = 4
PE_TAPS = (CENTRE, 3, 5, 1)
SLOT = L
SLOTS = 12
LN_EXP = "natural_log_exp_and_others"
EXTRA = 3072


def window(tap, r0, r1):
    dy, dx = tap // 3 - 1, tap % 3 - 1
    ya, yb = max(r0, -dy), min(r1, H - dy)
    xa, xb = max(0, -dx), min(W, W - dx)
    return (ya, yb, xa, xb), (ya + dy, yb + dy, xa + dx, xb + dx)


class Stage:

    held, turn = None, 0

    def __init__(self, nc, *names, repeats=False):
        self.nc, self.names, self.repeats, self.stack = nc, names, repeats, ExitStack()

    def __enter__(self):
        Stage.turn = 1 - Stage.turn
        self.sems = [self.stack.enter_context(self.nc.semaphore(f"{n}_{'ab'[Stage.turn]}")) for n in self.names]
        return self.sems

    def __exit__(self, *e):
        if e[0] is None:
            numbers = sorted(s.num for s in self.sems)
            first = 0
            for i in range(1, len(numbers) + 1):
                if i == len(numbers) or numbers[i] != numbers[i - 1] + 1:
                    self.nc.gpsimd.sem_clear(range(numbers[first], numbers[i - 1] + 1))
                    first = i
            if self.repeats:
                self.nc.all_engine_barrier()
        if Stage.held is not None:
            Stage.held.close()
        Stage.held = self.stack


class Chip:

    def __init__(self, nc, ctx):
        def sb(name, shape, dt=F32):
            return ctx.enter_context(nc.sbuf_tensor(name, shape, dt))

        self.nc = nc
        self.arena = sb("arena", [128, SLOTS * SLOT + EXTRA])
        self.ps = ctx.enter_context(nc.psum_tensor("ps", [128, 8, T], F32))
        self.ident = sb("ident", [128, 128])
        self.sel = sb("sel", [P, 32], BF16)
        self.eps = sb("eps", [128, 1])
        self.group = sb("group", [P, P])
        self.gn_stats = sb("gn_stats", [P, NH, NT * 6])
        self.gn_mean = sb("gn_mean", [P, NH])
        self.gn_rstd = sb("gn_rstd", [P, NH])
        self.hist = sb("hist", [128, 5, 3])
        self.top = 0

    def slots(self, first, n, parts=128):
        return self.arena[0:parts, first * SLOT:(first + n) * SLOT].rearrange("p (t l) -> p t l", t=n)

    def start(self, slot):
        self.top = slot * SLOT

    def take(self, *shape, parts=128):
        n = 1
        for x in shape:
            n *= x
        a = self.arena[0:parts, self.top:self.top + n]
        self.top += n
        assert self.top <= SLOTS * SLOT + EXTRA, self.top
        if len(shape) == 2:
            return a.rearrange("p (a b) -> p a b", a=shape[0])
        if len(shape) == 3:
            return a.rearrange("p (a b c) -> p a b c", a=shape[0], b=shape[1])
        return a


def constants(m):
    nc = m.nc
    with Stage(nc, "filled", "cut", "grouped") as (filled, cut, grouped), nc.Block() as block:
        @block.gpsimd
        def _(pool):
            nc.gpsimd.memset(m.ident[:, :], 0.0).then_inc(filled, 1)
            nc.gpsimd.memset(m.sel[:, :], 0.0).then_inc(filled, 1)
            nc.gpsimd.memset(m.eps[:, :], 1e-5)
            pool.wait_ge(filled, 2)
            nc.gpsimd.affine_select(out=m.ident[:, :], in_=m.ident[:, :], compare_op=ALU.not_equal, fill=1.0,
                                    base=0, pattern=[[-1, 128]], channel_multiplier=1)
            for i in range(3):
                nc.gpsimd.affine_select(out=m.sel[:, :], in_=m.sel[:, :], compare_op=ALU.not_equal, fill=1.0,
                                        base=-32 * i, pattern=[[-1, 32]], channel_multiplier=1).then_inc(cut, 1)
                pool.wait_ge(cut, i + 1)
            nc.gpsimd.memset(m.group[:, :], 1.0 / GROUP).then_inc(grouped, 1)
            g3 = m.group[:, :].rearrange("p (g c) -> p g c", c=GROUP)
            for i, (base, step) in enumerate(((0, 1), (GROUP - 1, -1))):
                pool.wait_ge(grouped, i + 1)
                nc.gpsimd.affine_select(out=g3, in_=g3, compare_op=ALU.is_ge, fill=0.0, base=base,
                                        pattern=[[-GROUP * step, P // GROUP], [0, GROUP]], channel_multiplier=step).then_inc(grouped, 1)


def bring(m, sp, brought, loads):
    with m.nc.allow_non_contiguous_dma(reason="columns of small vectors"):
        for dst, src in loads:
            sp.dma_start(dst, src).then_inc(brought, 16)
    if loads:
        sp.wait_ge(brought, 16 * len(loads))


def block_stats(m, x, half, i):
    return m.nc.vector.bn_stats(m.gn_stats[:, half, bass.ds(i * 6, 6)], x)


def group_norm(m, src, dst, taps, load=None, loads=(), have_stats=False):
    nc = m.nc
    m.start(10)
    mv = m.take(NH, 2, parts=P)
    dev = m.take(NH, parts=P)
    names = ("loaded_0", "loaded_1", "stats_done", "mean_mm", "var_in", "var_mm", "chain", "rstd_in", "rstd_out",
             "brought") + Taps.NAMES
    with Stage(nc, *names) as (*loaded, stats_done, mean_mm, var_in, var_mm, chain, rstd_in, rstd_out, brought,
                               taps_loaded, centre), nc.Block() as block:
        @block.sync
        def _(sp):
            for h in range(NH):
                if load is not None:
                    sp.dma_start(src[:, h, :], load[:, h, :]).then_inc(loaded[h], 16)
            taps.sync(sp, taps_loaded)
            bring(m, sp, brought, loads)

        @block.gpsimd
        def _(pool):
            taps.gpsimd(pool, taps_loaded, centre)

        @block.vector
        def _(dve):
            n = 0

            def link(ins):
                nonlocal n
                n += 1
                ins.then_inc(chain, 1)
                dve.wait_ge(chain, n)

            for h in range(NH):
                if load is not None:
                    dve.wait_ge(loaded[h], 16)
                if not have_stats:
                    for i in range(NT):
                        ins = block_stats(m, src[:, h, i * T:(i + 1) * T], h, i)
                    link(ins)
                link(nc.vector.bn_aggr(mv[:, h, :], m.gn_stats[:, h, :]))
            nc.vector.tensor_copy(dev, mv[:, :, 0]).then_inc(stats_done, 1)
            dve.wait_ge(mean_mm, 1)
            link(nc.vector.tensor_copy(m.gn_mean[:, :], m.ps[0:P, 0, 0:NH]))
            link(nc.vector.tensor_tensor(dev, dev, m.gn_mean[:, :], ALU.subtract))
            link(nc.vector.tensor_tensor(dev, dev, dev, ALU.mult))
            nc.vector.tensor_tensor(dev, dev, mv[:, :, 1], ALU.add).then_inc(var_in, 1)
            dve.wait_ge(var_mm, 1)
            nc.vector.tensor_scalar(m.gn_rstd[:, :], m.ps[0:P, 1, 0:NH], 1e-5, None, ALU.add).then_inc(rstd_in, 1)
            dve.wait_ge(rstd_out, 1)
            link(nc.vector.reciprocal(m.gn_rstd[:, :], m.gn_rstd[:, :]))
            for h in range(NH):
                nc.vector.tensor_scalar(dst[:, h, :], src[:, h, :], m.gn_mean[:, h:h + 1], m.gn_rstd[:, h:h + 1],
                                        ALU.subtract, ALU.mult)

        @block.scalar
        def _(act):
            act.wait_ge(rstd_in, 1)
            nc.scalar.activation(m.gn_rstd[:, :], m.gn_rstd[:, :], ACT.Sqrt).then_inc(rstd_out, 1)

        @block.tensor
        def _(pe):
            pe.wait_ge(stats_done, 1)
            nc.tensor.matmul(m.ps[0:P, 0, 0:NH], m.group[:, :], dev, start=True, stop=True).then_inc(mean_mm, 1)
            pe.wait_ge(var_in, 1)
            nc.tensor.matmul(m.ps[0:P, 1, 0:NH], m.group[:, :], dev, start=True, stop=True).then_inc(var_mm, 1)


class Taps:

    NAMES = ("taps_loaded", "centre")

    def __init__(self, m, n, parts, weight, bias, own=False, slot=SLOTS):
        self.m, self.n, self.parts, self.weight, self.bias, self.own = m, n, parts, weight, bias, own
        m.start(slot)
        self.w = m.take(n, 9, parts=parts)
        self.b = m.take(n, parts=parts)
        self.diag = m.take(n * len(PE_TAPS), parts, parts=parts)

    def sync(self, sp, loaded):
        nc = self.m.nc
        sp.dma_start(self.w, self.weight.rearrange("(t p) k -> p t k", p=self.parts)).then_inc(loaded, 16)
        with nc.allow_non_contiguous_dma(reason="a few words a partition"):
            sp.dma_start(self.b, columns(self.bias, self.parts)).then_inc(loaded, 16)

    def gpsimd(self, pool, loaded, centre):
        nc, w = self.m.nc, self.w
        pool.wait_ge(loaded, 32)
        if self.own:
            nc.gpsimd.tensor_scalar(w[:, :, 4:5], w[:, :, 4:5], 1.0, None, ALU.add).then_inc(centre, 1)
            pool.wait_ge(centre, 1)
        for t in range(self.n):
            for i, tap in enumerate(PE_TAPS):
                nc.gpsimd.tensor_scalar(self.diag[:, t * len(PE_TAPS) + i, :], self.m.ident[0:self.parts, 0:self.parts],
                                        w[:, t, tap:tap + 1], None, ALU.mult)


def conv3x3(m, src, dst, taps, residual=None, silu=False, out=None, loads=()):
    nc, n, parts = m.nc, taps.n, taps.parts
    w, bcol, diag = taps.w, taps.b, taps.diag
    steps = [(t, r) for t in range(n) for r in range(0, H, ROWS)]
    src4 = src.rearrange("p t (h w) -> p t h w", w=W)
    dst4 = dst.rearrange("p t (h w) -> p t h w", w=W)
    last = len(steps) - 1

    def pe_taps(i):
        return () if i == 0 else PE_TAPS[:3] if i <= 2 else PE_TAPS

    def dve_taps(i):
        return [tap for tap in range(9) if tap not in pe_taps(i)]

    halved = {i: [(i, steps[i][1] + half * ROWS // 2, ROWS // 2) for half in range(2)] for i in (0, last)}
    groups = [halved[0]] + [[(i, steps[i][1], ROWS), (i + 1, steps[i + 1][1], ROWS)] for i in range(1, last, 2)] + [halved[last]]
    tapped_all = {}
    count = 0
    for group in groups:
        count += 2 * len(dve_taps(group[0][0]))
        for piece, (i, _, _) in enumerate(group):
            tapped_all[i] = count - 1 + piece

    def rows(v, t, r):
        return v[:, t, r * W:(r + ROWS) * W]

    with Stage(nc, "taps_mm", "taken", "tapped", "whole", "stored", "brought") as (taps_mm, taken, tapped, whole, stored,
                                                                                    brought), nc.Block() as block:
        @block.sync
        def _(sp):
            bring(m, sp, brought, loads)
            if out is not None:
                for i, (t, r) in enumerate(steps):
                    sp.wait_ge(whole, i + 1)
                    sp.dma_start(rows(out, t, r), rows(dst, t, r)).then_inc(stored, 16)
                sp.wait_ge(stored, 16 * len(steps))

        if residual is not None:
            @block.gpsimd
            def _(pool):
                for i, (t, r) in enumerate(steps):
                    pool.wait_ge(tapped, tapped_all[i])
                    nc.gpsimd.tensor_tensor(rows(dst, t, r), rows(dst, t, r), rows(residual, t, r), ALU.add).then_inc(whole, 1)

        @block.tensor
        def _(pe):
            for i in range(1, len(steps)):
                t, r = steps[i]
                if i >= 5:
                    pe.wait_ge(taken, i - 4)
                for half in range(2):
                    r0 = r + half * ROWS // 2
                    out = m.ps[0:parts, (2 * i + half) % 8, :].rearrange("p (h w) -> p h w", w=W)
                    for j, tap in enumerate(pe_taps(i)):
                        (ya, yb, xa, xb), (sa, sb_, ca, cb) = window(tap, r0, r0 + ROWS // 2)
                        ins = nc.tensor.matmul(out[:, ya - r0:yb - r0, xa:xb], diag[:, t * len(PE_TAPS) + j, :],
                                               src4[:, t, sa:sb_, ca:cb], start=(j == 0), stop=(j == len(pe_taps(i)) - 1))
                ins.then_inc(taps_mm, 1)

        @block.scalar
        def _(act):
            def finish(i):
                t, r = steps[i]
                act.wait_ge(tapped, tapped_all[i])
                nc.scalar.activation(rows(dst, t, r), rows(dst, t, r), ACT.Silu, bias=0.0 if i == 0 else bcol[:, t:t + 1])

            for i in range(1, len(steps)):
                t, r = steps[i]
                act.wait_ge(taps_mm, i)
                both = m.ps[0:parts, (2 * i) % 8:(2 * i) % 8 + 2, :]
                out = rows(dst, t, r).rearrange("p (a b) -> p a b", a=2)
                if silu:
                    nc.scalar.copy(out, both).then_inc(taken, 1)
                    if i >= 4:
                        finish(i - 4)
                else:
                    nc.scalar.activation(out, both, ACT.Identity, bias=bcol[:, t:t + 1]).then_inc(taken, 1)
            if silu:
                for i in range(last - 3, last + 1):
                    finish(i)

        @block.vector
        def _(dve):
            before = 0
            for group in groups:
                for j in range(len(dve_taps(group[0][0]))):
                    for piece, (i, r, height) in enumerate(group):
                        t, tap = steps[i][0], dve_taps(i)[j]
                        if i == 0:
                            tap = CENTRE if j == 0 else tap - 1 if j <= CENTRE else tap
                        if j:
                            dve.wait_ge(tapped, before + 2 * j - 1 + piece)
                        elif i:
                            dve.wait_ge(taken, i)
                        (ya, yb, xa, xb), (sa, sb_, ca, cb) = window(tap, r, r + height)
                        o, x, wcol = dst4[:, t, ya:yb, xa:xb], src4[:, t, sa:sb_, ca:cb], w[:, t, tap:tap + 1]
                        if i == 0 and j == 0:
                            ins = nc.vector.tensor_scalar(o, x, wcol, bcol[:, t:t + 1], ALU.mult, ALU.add)
                        else:
                            ins = nc.vector.scalar_tensor_tensor(o, x, wcol, o, ALU.mult, ALU.add)
                        ins.then_inc(tapped, 1)
                before += 2 * len(dve_taps(group[0][0]))


class LayerNorm:

    NAMES = ("ln_mean", "ln_centred", "ln_squared", "ln_var", "ln_log", "ln_rstd", "ln_scaled", "ln_out")

    def __init__(self, m, n, parts, wcol, bcol, which=""):
        self.m, self.n, self.parts, self.wcol, self.bcol, self.which = m, n, parts, wcol, bcol, which
        self.xc = m.take(n, T, parts=parts)
        self.sq = m.take(n, T, parts=parts)
        self.rstd = m.take(T, parts=parts)
        self.mean_of = m.take(parts, parts=parts)
        self.names = [self.key(x) for x in self.NAMES]

    def key(self, name):
        return name + self.which

    def constants(self):
        return self.m.nc.vector.memset(self.mean_of, 1.0 / (self.n * self.parts))

    def pe_mean(self, pe, s, x, bank=0):
        nc, ps = self.m.nc, self.m.ps
        for t in range(self.n):
            ins = nc.tensor.matmul(ps[0:self.parts, bank, :], self.mean_of, x[:, t, :], start=(t == 0), stop=(t == self.n - 1))
        ins.then_inc(s[self.key("ln_mean")], 1)

    def pe_var(self, pe, s, bank=1):
        nc, ps = self.m.nc, self.m.ps
        for t in range(self.n):
            pe.wait_ge(s[self.key("ln_squared")], t + 1)
            ins = nc.tensor.matmul(ps[0:self.parts, bank, :], self.mean_of, self.sq[:, t, :], start=(t == 0), stop=(t == self.n - 1))
        ins.then_inc(s[self.key("ln_var")], 1)

    def dve_centre(self, dve, s, x, bank=0):
        nc, ps = self.m.nc, self.m.ps
        dve.wait_ge(s[self.key("ln_mean")], 1)
        for t in range(self.n):
            nc.vector.tensor_tensor(self.xc[:, t, :], x[:, t, :], ps[0:self.parts, bank, :], ALU.subtract).then_inc(
                s[self.key("ln_centred")], 1)

    def dve_scale(self, dve, s):
        nc = self.m.nc
        dve.wait_ge(s[self.key("ln_rstd")], 1)
        dve.wait_ge(s[self.key("ln_centred")], self.n)
        for t in range(self.n):
            nc.vector.tensor_tensor(self.xc[:, t, :], self.xc[:, t, :], self.rstd, ALU.mult).then_inc(s[self.key("ln_scaled")], 1)

    def act_square(self, act, s):
        nc = self.m.nc
        for t in range(self.n):
            act.wait_ge(s[self.key("ln_centred")], t + 1)
            nc.scalar.square(self.sq[:, t, :], self.xc[:, t, :]).then_inc(s[self.key("ln_squared")], 1)

    def act_rstd(self, act, s, bank):
        nc, ps = self.m.nc, self.m.ps
        act.wait_ge(s[self.key("ln_var")], 1)
        nc.scalar.activation(self.rstd, ps[0:self.parts, bank, :], ACT.Ln, bias=self.m.eps[0:self.parts, :]).then_inc(
            s[self.key("ln_log")], 1)
        act.wait_ge(s[self.key("ln_log")], 1)
        nc.scalar.activation(self.rstd, self.rstd, ACT.Exp, scale=-0.5).then_inc(s[self.key("ln_rstd")], 1)

    def act_out(self, act, s, out):
        nc = self.m.nc
        for t in range(self.n):
            act.wait_ge(s[self.key("ln_scaled")], t + 1)
            nc.scalar.activation(out[:, t, :], self.xc[:, t, :], ACT.Identity, scale=self.wcol[:, t:t + 1],
                                 bias=self.bcol[:, t:t + 1]).then_inc(s[self.key("ln_out")], 1)


def columns(vector, parts):
    return vector.rearrange("(t p) -> p t", p=parts)


def mlp_weights(m, a):
    m.start(6)
    w1 = m.take(NH, MLP, parts=P)
    w2 = m.take(NM, C)
    b1 = m.take(NM)
    cols = m.take(3, NH, parts=P)
    loads = [(w1, a["fc1_w"].rearrange("(t p) o -> p t o", p=P)), (w2, a["fc2_w"].rearrange("(t p) o -> p t o", p=128)),
             (b1, columns(a["fc1_b"], 128)), (cols[:, 0, :], columns(a["ln2_w"], P)),
             (cols[:, 1, :], columns(a["ln2_b"], P)), (cols[:, 2, :], columns(a["fc2_b"], P))]
    return (w1, w2, b1, cols), loads


def mlp(m, x2, x, weights):
    nc = m.nc
    w1, w2, b1, cols = weights
    lns = [LayerNorm(m, NH, P, cols[:, 0, :], cols[:, 1, :], "ab"[i]) for i in range(2)]
    xin = [m.take(NH, T, parts=P) for _ in range(2)]
    h = [m.take(NH, T, parts=P) for _ in range(2)]
    g = [m.take(NM, T) for _ in range(2)]
    names = ["taken", "fc1_mm", "gelu_done", "fc2_mm", "added", "summed", "filled"] + lns[0].names + lns[1].names

    def step(back, front, repeats=False):
        def tokens(v, pair, i):
            return v[:, :, bass.ds((2 * pair + i) * T, T)]

        with Stage(nc, *names, repeats=repeats) as sems, nc.Block() as block:
            at = dict(zip(names, sems))
            taken, fc1_mm, gelu_done, fc2_mm, added, summed, filled = sems[:7]

            @block.scalar
            def _(act):
                if front is not None:
                    for i in range(2):
                        nc.scalar.copy(xin[i], tokens(x2, front, i)).then_inc(taken, 1)
                if back is not None:
                    for u in range(2 * NM):
                        if u == 2 * NM - 2 and front is not None:
                            lns[0].act_square(act, at)
                        act.wait_ge(fc1_mm, u + 1)
                        nc.scalar.activation(g[u // NM][:, u % NM, :], m.ps[:, 2 + u % 4, :], ACT.Gelu,
                                             bias=b1[:, u % NM:u % NM + 1]).then_inc(gelu_done, 1)
                if front is not None:
                    nc.scalar.preload_act_table_set(LN_EXP)
                    if back is None:
                        lns[0].act_square(act, at)
                    lns[0].act_rstd(act, at, 1)
                    lns[1].act_square(act, at)
                    lns[0].act_out(act, at, h[0])
                    lns[1].act_rstd(act, at, 1)
                    lns[1].act_out(act, at, h[1])

            @block.tensor
            def _(pe):
                def fc1(i, o):
                    u = i * NM + o
                    if u >= 4:
                        pe.wait_ge(gelu_done, u - 3)
                    for t in range(NH):
                        ins = nc.tensor.matmul(m.ps[:, 2 + u % 4, :], w1[:, t, o * 128:(o + 1) * 128], h[i][:, t, :],
                                               start=(t == 0), stop=(t == NH - 1))
                    ins.then_inc(fc1_mm, 1)

                def fc2(i, c):
                    if i:
                        pe.wait_ge(summed, c + 1)
                    for o in range(NM):
                        pe.wait_ge(gelu_done, i * NM + o + 1)
                        ins = nc.tensor.matmul(m.ps[0:P, 6 + c, :], w2[:, o, c * P:(c + 1) * P], g[i][:, o, :],
                                               start=(o == 0), stop=(o == NM - 1))
                    ins.then_inc(fc2_mm, 1)

                def mean(i):
                    if i:
                        pe.wait_ge(at[lns[0].key("ln_centred")], NH)
                    pe.wait_ge(taken, i + 1)
                    lns[i].pe_mean(pe, at, xin[i], 0)

                def var(i):
                    if i:
                        pe.wait_ge(at[lns[0].key("ln_log")], 1)
                    lns[i].pe_var(pe, at, 1)

                if back is not None:
                    for o in range(NM):
                        fc1(0, o)
                    for c in range(NH):
                        fc2(0, c)
                    for o in range(NM - 2):
                        fc1(1, o)
                if back is None:
                    pe.wait_ge(filled, 2)
                if front is not None:
                    mean(0)
                if back is not None:
                    for o in range(NM - 2, NM):
                        fc1(1, o)
                if front is not None:
                    var(0)
                    mean(1)
                if back is not None:
                    fc2(1, 0)
                if front is not None:
                    var(1)
                if back is not None:
                    fc2(1, 1)

            @block.vector
            def _(dve):
                if back is None:
                    for one in lns:
                        one.constants().then_inc(filled, 1)

                def add_up(i, c):
                    n = i * NH + c
                    blk = tokens(x, back, i)[:, c, :]
                    nc.vector.scalar_tensor_tensor(blk, tokens(x2, back, i)[:, c, :], cols[:, 2, c:c + 1], blk,
                                                   ALU.add, ALU.add).then_inc(added, 1)
                    dve.wait_ge(fc2_mm, n + 1)
                    dve.wait_ge(added, n + 1)
                    nc.vector.tensor_tensor(blk, m.ps[0:P, 6 + c, :], blk, ALU.add).then_inc(summed, 1)
                    dve.wait_ge(summed, n + 1)
                    block_stats(m, blk, c, 2 * back + i)

                if back is not None:
                    add_up(0, 0)
                    add_up(0, 1)
                if front is not None:
                    lns[0].dve_centre(dve, at, xin[0], 0)
                    lns[1].dve_centre(dve, at, xin[1], 0)
                    lns[0].dve_scale(dve, at)
                if back is not None:
                    add_up(1, 0)
                if front is not None:
                    lns[1].dve_scale(dve, at)
                if back is not None:
                    add_up(1, 1)

    step(None, 0)
    with nc.Fori(0, NT // 2 - 1) as s:
        step(s, s + 1, repeats=True)
    step(NT // 2 - 1, None)


def ssd_weights(m, a):
    m.start(6)
    w = {"zdt": m.take(NH, DIN0, parts=P), "xbc": m.take(NH, D2 + 2 * DS, parts=P), "out": m.take(N2, C),
         "ln": m.take(2, NH, parts=P), "conv": m.take(5, 4), "conv_bias": m.take(5), "rms": m.take(N2),
         "dt_bias": m.take(HEADS), "neg_a": m.take(HEADS), "skip": m.take(HEADS)}
    in_w = a["in_proj_w"].rearrange("(t p) o -> p t o", p=P)
    cwd = a["conv1d_w"]
    cbd = a["conv1d_b"].rearrange("(a c) -> a c", c=1)
    loads = [(w["zdt"][:, :, 0:D2], in_w[:, :, 0:D2]), (w["zdt"][:, :, D2:DIN0], in_w[:, :, 2 * D2 + 2 * DS:]),
             (w["xbc"], in_w[:, :, D2:2 * D2 + 2 * DS]), (w["out"], a["out_proj_w"].rearrange("(t p) o -> p t o", p=128)),
             (w["ln"][:, 0, :], columns(a["ln1_w"], P)), (w["ln"][:, 1, :], columns(a["ln1_b"], P)),
             (w["conv"][:, 0:3, :], cwd[0:D2, :].rearrange("(t p) k -> p t k", p=128)),
             (w["conv"][0:DS, 3, :], cwd[D2:D2 + DS, :]), (w["conv"][0:DS, 4, :], cwd[D2 + DS:, :]),
             (w["conv_bias"][:, 0:3], columns(a["conv1d_b"][0:D2], 128)), (w["conv_bias"][0:DS, 3:4], cbd[D2:D2 + DS, :]),
             (w["conv_bias"][0:DS, 4:5], cbd[D2 + DS:, :]), (w["rms"], columns(a["rms_w"], 128)),
             (w["dt_bias"], a["dt_bias"].partition_broadcast(128)), (w["neg_a"], a["A_log"].partition_broadcast(128)),
             (w["skip"], a["D_skip"].partition_broadcast(128))]
    return w, loads


def ssd(m, xs, weights, taps):
    nc = m.nc
    w_zdt, w_xbc, w_out, lncol, cw, cb, rms, dt_bias, neg_a, skip = weights.values()
    upto = m.take(Q)
    after = m.take(Q)
    ones = m.take(Q)
    ln = LayerNorm(m, NH, P, lncol[:, 0, :], lncol[:, 1, :])
    dtr = m.take(NQ * HEADS)
    dte = m.take(NQ * HEADS)
    dtw = m.take(NQ * HEADS)
    dtl = m.take(NQ * HEADS)
    xbc_of = [m.take(5, T) for _ in range(2)]
    zdt_of = [m.take(NQ, DIN0) for _ in range(2)]
    dt_of = [m.take(NQ * HEADS) for _ in range(2)]
    da_of = [m.take(NQ, HEADS) for _ in range(2)]
    dec_of = [m.take(3, NQ, HEADS) for _ in range(2)]
    xtok = m.take(NQ, D2 + DS)
    xdl = m.take(NQ, D2)
    r = m.take(2, HEADS * Q)
    e = m.take(2, HEADS * Q)
    cbm = m.take(2, Q)
    y = m.take(NQ, D2)
    ss = m.take(NQ)
    product = m.take(T)
    assert m.top <= SLOTS * SLOT
    m.start(2)
    xb = m.take(5, 3 + T)
    xin = m.take(NH, T, parts=P)
    h = m.take(NH, T, parts=P)
    xdt = m.take(NQ, D2)
    yt = m.take(N2, T)
    state = m.take(D2, parts=DS)
    assert m.top <= 4 * SLOT
    with Stage(nc, "filled", "negated", *Taps.NAMES) as (filled, negated, taps_loaded, centre), nc.Block() as block:
        @block.sync
        def _(sp):
            taps.sync(sp, taps_loaded)

        @block.vector
        def _(dve):
            ln.constants()

        @block.scalar
        def _(act):
            nc.scalar.activation(neg_a, neg_a, ACT.Exp).then_inc(negated, 1)
            act.wait_ge(negated, 1)
            nc.scalar.mul(neg_a, neg_a, -1.0)
            for t in range(N2):
                nc.scalar.activation(w_out[:, t, :], w_out[:, t, :], ACT.Copy, scale=rms[:, t:t + 1])

        @block.gpsimd
        def _(pool):
            nc.gpsimd.memset(upto, 1.0).then_inc(filled, 1)
            nc.gpsimd.memset(after, 1.0).then_inc(filled, 1)
            nc.gpsimd.memset(ones, 1.0)
            nc.gpsimd.memset(state, 0.0)
            nc.gpsimd.memset(m.hist[:, :, :], 0.0)
            pool.wait_ge(filled, 2)
            nc.gpsimd.affine_select(out=upto, in_=upto, compare_op=ALU.is_ge, fill=0.0, base=0,
                                    pattern=[[1, Q]], channel_multiplier=-1)
            nc.gpsimd.affine_select(out=after, in_=after, compare_op=ALU.is_gt, fill=0.0, base=0,
                                    pattern=[[-1, Q]], channel_multiplier=1)
            taps.gpsimd(pool, taps_loaded, centre)

    def heads(v, n=HD):
        return v.rearrange("p (h o) -> p h o", o=1).broadcast_to([v.shape[0], HEADS, n])

    def by_head(v):
        return v.rearrange("p (h d) -> p h d", h=HEADS)

    parts_of = (128, 128, 128, DS, DS)
    offs = (0, 128, 256, D2, D2 + DS)
    names = ("taken", "zdt_mm", "zdt_in", "xbc_mm", "xbc_in", "conv_first", "conv_tap", "conv_pool", "dt_in", "dt_step",
             "dt_done", "da_done", "sums_mm", "decays", "tok_mm", "tok_out", "xdt_done", "xdl_done", "r_done", "seg_mm",
             "e_done", "cb_mm", "cbm_done", "scored_done", "y_mm", "y_read", "inter_mm", "state_mm", "state_done",
             "y_step", "y_gated", "rms_log", "rms_rstd", "y_normed", "yt_mm", "yt_out", "out_mm", "out_added",
             "skipped") + LayerNorm.NAMES

    def block_of(i):
        return xs[:, :, bass.ds(i * T, T)]


    def front_scalar(act, at, i, par, step, q=None):
        xbc, zdt = xbc_of[par], zdt_of[par]
        if step == "take":
            nc.scalar.copy(xin, block_of(i)).then_inc(at["taken"], 1)
        elif step == "square":
            ln.act_square(act, at)
        elif step == "rstd":
            ln.act_rstd(act, at, 7)
        elif step == "norm":
            ln.act_out(act, at, h)
        elif step == "zdt":
            act.wait_ge(at["zdt_mm"], q + 1)
            nc.scalar.copy(zdt[:, q, :], m.ps[:, 6 + q % 2, 0:DIN0]).then_inc(at["zdt_in"], 1)
        elif step == "dt":
            act.wait_ge(at["dt_in"], 1)
            nc.scalar.activation(dte, dtr, ACT.Abs).then_inc(at["dt_step"], 1)
            act.wait_ge(at["dt_step"], 1)
            nc.scalar.activation(dte, dte, ACT.Exp, scale=-1.0).then_inc(at["dt_step"], 1)
            act.wait_ge(at["dt_step"], 2)
            nc.scalar.activation(dtw, dte, ACT.Identity, bias=1.0).then_inc(at["dt_step"], 1)
            act.wait_ge(at["dt_step"], 3)
            nc.scalar.activation(dtl, dtw, ACT.Ln).then_inc(at["dt_step"], 1)
        elif step == "history":
            nc.scalar.copy(xb[:, :, 0:3], m.hist[:, :, :])
        elif step == "xbc":
            n = parts_of[q]
            act.wait_ge(at["xbc_mm"], q + 1)
            nc.scalar.copy(xb[0:n, q, 3:], m.ps[0:n, 6 + q % 2, :]).then_inc(at["xbc_in"], 1)
            act.wait_ge(at["xbc_in"], q + 1)
            nc.scalar.activation(xbc[0:n, q, :], xb[0:n, q, 0:T], ACT.Copy, scale=cw[0:n, q, 0:1]).then_inc(at["conv_first"], 1)
        elif step == "decays":
            act.wait_ge(at["sums_mm"], 1)
            nc.scalar.activation(dec_of[par], m.ps[:, 7, 0:3 * NQ * HEADS].rearrange("p (a q h) -> p a q h", a=3, q=NQ),
                                 ACT.Exp).then_inc(at["decays"], 1)
        elif step == "silu":
            nc.scalar.activation(zdt[:, :, 0:D2], zdt[:, :, 0:D2], ACT.Silu)
            for j, n in enumerate(parts_of):
                if j == 0:
                    act.wait_ge(at["conv_pool"], 6)
                else:
                    act.wait_ge(at["conv_tap"], 3 * j)
                nc.scalar.activation(xbc[0:n, j, :], xbc[0:n, j, :], ACT.Silu, bias=cb[0:n, j:j + 1])

    def front_tensor(pe, at, i, par, step, q=None):
        if step == "mean":
            pe.wait_ge(at["taken"], 1)
            ln.pe_mean(pe, at, xin, 6)
        elif step == "var":
            ln.pe_var(pe, at, 7)
        elif step == "zdt":
            if q == 0:
                pe.wait_ge(at["ln_out"], NH)
            if q >= 2:
                pe.wait_ge(at["zdt_in"], q - 1)
            for t in range(NH):
                ins = nc.tensor.matmul(m.ps[:, 6 + q % 2, 0:DIN0], h[:, t, q * Q:(q + 1) * Q], w_zdt[:, t, :],
                                       start=(t == 0), stop=(t == NH - 1))
            ins.then_inc(at["zdt_mm"], 1)
        elif step == "xbc":
            n = parts_of[q]
            if q < 2:
                pe.wait_ge(at["zdt_in"], NQ - 1 + q)
            elif q == 3:
                pe.wait_ge(at["decays"], 1)
            else:
                pe.wait_ge(at["xbc_in"], q - 1)
            for t in range(NH):
                ins = nc.tensor.matmul(m.ps[0:n, 6 + q % 2, :], w_xbc[:, t, offs[q]:offs[q] + n], h[:, t, :],
                                       start=(t == 0), stop=(t == NH - 1))
            ins.then_inc(at["xbc_mm"], 1)
        elif step == "sums":
            pe.wait_ge(at["da_done"], 1)
            pe.wait_ge(at["xbc_in"], 2)
            for j, lhs in enumerate((upto, after, ones)):
                ins = nc.tensor.matmul(m.ps[:, 7, j * NQ * HEADS:(j + 1) * NQ * HEADS], lhs,
                                       da_of[par].rearrange("p q h -> p (q h)"), start=True, stop=True)
            ins.then_inc(at["sums_mm"], 1)

    def front_vector(dve, at, i, par, step, q=None):
        if step == "centre":
            ln.dve_centre(dve, at, xin, 6)
        elif step == "scale":
            ln.dve_scale(dve, at)
        elif step == "dt_in":
            dve.wait_ge(at["zdt_in"], NQ)
            nc.vector.tensor_tensor(dtr.rearrange("p (q h) -> p q h", q=NQ), zdt_of[par][:, :, D2:DIN0],
                                    dt_bias.rearrange("p (o h) -> p o h", o=1).broadcast_to([128, NQ, HEADS]),
                                    ALU.add).then_inc(at["dt_in"], 1)
        elif step == "dt":
            dve.wait_ge(at["dt_step"], 4)
            nc.vector.scalar_tensor_tensor(dtw, dtw, 1.0, dte, ALU.subtract, ALU.subtract).then_inc(at["dt_done"], 1)
            dve.wait_ge(at["dt_done"], 1)
            nc.vector.tensor_tensor(dtl, dtl, dtw, ALU.subtract).then_inc(at["dt_done"], 1)
            dve.wait_ge(at["dt_done"], 2)
            nc.vector.scalar_tensor_tensor(dt_of[par], dtr, 0.0, dtl, ALU.max, ALU.add).then_inc(at["dt_done"], 1)
            dve.wait_ge(at["dt_done"], 3)
            nc.vector.tensor_tensor(da_of[par], dt_of[par].rearrange("p (q h) -> p q h", q=NQ),
                                    neg_a.rearrange("p (o h) -> p o h", o=1).broadcast_to([128, NQ, HEADS]),
                                    ALU.mult).then_inc(at["da_done"], 1)
        elif step == "conv":
            n, xbc = parts_of[q], xbc_of[par]
            dve.wait_ge(at["conv_first"], q + 1)
            for k in range(1, 4):
                if k > 1:
                    dve.wait_ge(at["conv_tap"], 3 * (q - 1) + k - 1)
                nc.vector.scalar_tensor_tensor(xbc[0:n, q, :], xb[0:n, q, k:k + T], cw[0:n, q, k:k + 1], xbc[0:n, q, :],
                                               ALU.mult, ALU.add).then_inc(at["conv_tap"], 1)
            nc.vector.tensor_copy(m.hist[0:n, q, :], xb[0:n, q, T:T + 3])

    def front_gpsimd(pool, at, par):
        xbc = xbc_of[par]
        pool.wait_ge(at["conv_first"], 1)
        for k in range(1, 4):
            if k > 1:
                pool.wait_ge(at["conv_pool"], 2 * (k - 1))
            nc.gpsimd.tensor_scalar(product, xb[:, 0, k:k + T], cw[:, 0, k:k + 1], None, ALU.mult).then_inc(at["conv_pool"], 1)
            pool.wait_ge(at["conv_pool"], 2 * k - 1)
            nc.gpsimd.tensor_tensor(xbc[:, 0, :], xbc[:, 0, :], product, ALU.add).then_inc(at["conv_pool"], 1)
        nc.gpsimd.tensor_copy(m.hist[:, 0, :], xb[:, 0, T:T + 3])


    def back_scalar(act, at, i, par, step, q=None):
        if step == "tok":
            act.wait_ge(at["tok_mm"], q + 1)
            nc.scalar.copy(xtok[:, q, :], m.ps[:, q % 2, 0:D2 + DS]).then_inc(at["tok_out"], 1)
        elif step == "e":
            act.wait_ge(at["seg_mm"], q + 1)
            if q >= 2:
                act.wait_ge(at["scored_done"], q - 1)
            nc.scalar.activation(e[:, q % 2, :].rearrange("p (a b) -> p a b", b=HEADS * Q // 2),
                                 m.ps[:, 2:4, 0:HEADS * Q // 2], ACT.Exp).then_inc(at["e_done"], 1)
        elif step == "square":
            act.wait_ge(at["y_gated"], q + 1)
            nc.scalar.activation(xdl[:, q, :], y[:, q, :], ACT.Square, accum_out=ss[:, q:q + 1])

    def back_tensor(pe, at, i, par, step, q=None):
        has_tail = not isinstance(i, int) or i > 0
        xbc = xbc_of[par]
        if step == "tok":
            if q >= 2:
                pe.wait_ge(at["tok_out"], q - 1)
            for j, n in enumerate(parts_of[:4]):
                ins = nc.tensor.transpose(m.ps[:, q % 2, offs[j]:offs[j] + n], xbc[0:n, j, q * Q:(q + 1) * Q],
                                          m.ident[0:n, 0:n])
            ins.then_inc(at["tok_mm"], 1)
        elif step == "seg":
            tok = slice(q * Q, (q + 1) * Q)
            if q >= 1:
                pe.wait_ge(at["e_done"], q)
            elif has_tail:
                pe.wait_ge(at["yt_out"], N2)
                pe.wait_ge(at["out_added"], NH)
            pe.wait_ge(at["r_done"], q + 1)
            for j in range(2):
                ins = nc.tensor.matmul(m.ps[:, 2 + j, 0:HEADS * Q // 2], after,
                                       r[:, q % 2, j * HEADS * Q // 2:(j + 1) * HEADS * Q // 2], start=True, stop=True)
            ins.then_inc(at["seg_mm"], 1)
            if q == 0:
                pe.wait_ge(at["tok_out"], NQ)
            else:
                pe.wait_ge(at["cbm_done"], q)
            nc.tensor.matmul(m.ps[:, 0, 0:Q], xbc[0:DS, 3, tok], xbc[0:DS, 4, tok], start=True, stop=True).then_inc(at["cb_mm"], 1)
            pe.wait_ge(at["xdl_done"], q + 1)
            if q >= 1:
                pe.wait_ge(at["state_done"], q)
            nc.tensor.matmul(m.ps[:, 5, 0:D2], xbc[0:DS, 4, tok], state, start=True, stop=True).then_inc(at["inter_mm"], 1)
            nc.tensor.matmul(m.ps[0:DS, 1, 0:D2], xtok[:, q, D2:D2 + DS], xdl[:, q, :], start=True, stop=True).then_inc(at["state_mm"], 1)
        elif step == "y":
            pe.wait_ge(at["scored_done"], q + 1)
            if q >= 1:
                pe.wait_ge(at["y_read"], q)
            for hd in range(HEADS):
                ins = nc.tensor.matmul(m.ps[:, 4, hd * HD:(hd + 1) * HD], e[:, q % 2, hd * Q:(hd + 1) * Q],
                                       xdt[:, q, hd * HD:(hd + 1) * HD], start=True, stop=True)
            ins.then_inc(at["y_mm"], 1)

    def back_vector(dve, at, i, par, step, q=None):
        has_tail = not isinstance(i, int) or i > 0
        zdt, dt, dec = zdt_of[par], dt_of[par], dec_of[par]
        if step == "xdt":
            dve.wait_ge(at["tok_out"], q + 1)
            nc.vector.tensor_tensor(by_head(xdt[:, q, :]), by_head(xtok[:, q, 0:D2]),
                                    heads(dt[:, q * HEADS:(q + 1) * HEADS]), ALU.mult).then_inc(at["xdt_done"], 1)
            dve.wait_ge(at["xdt_done"], q + 1)
            nc.vector.tensor_tensor(by_head(xdl[:, q, :]), by_head(xdt[:, q, :]), heads(dec[:, 1, q, :]),
                                    ALU.mult).then_inc(at["xdl_done"], 1)
        elif step == "score":
            dve.wait_ge(at["cb_mm"], q + 1)
            nc.vector.tensor_tensor(cbm[:, q % 2, :], m.ps[:, 0, 0:Q], upto, ALU.mult).then_inc(at["cbm_done"], 1)
            dve.wait_ge(at["cbm_done"], q + 1)
            dve.wait_ge(at["e_done"], q + 1)
            e3 = e[:, q % 2, :].rearrange("p (h i) -> p h i", h=HEADS)
            nc.vector.tensor_tensor(e3, e3, cbm[:, q % 2, :].rearrange("p (o i) -> p o i", o=1).broadcast_to([128, HEADS, Q]),
                                    ALU.mult).then_inc(at["scored_done"], 1)
            dve.wait_ge(at["inter_mm"], q + 1)
            nc.vector.tensor_tensor(by_head(state), by_head(state), heads(dec[0:DS, 2, q, :]), ALU.mult).then_inc(at["y_step"], 1)
            if q == 0 and has_tail:
                dve.wait_ge(at["yt_mm"], N2)
            nc.vector.tensor_tensor(by_head(y[:, q, :]), by_head(m.ps[:, 5, 0:D2]), heads(dec[:, 0, q, :]),
                                    ALU.mult).then_inc(at["y_step"], 1)
            dve.wait_ge(at["state_mm"], q + 1)
            dve.wait_ge(at["y_step"], 3 * q + 1)
            nc.vector.tensor_tensor(state, state, m.ps[0:DS, 1, 0:D2], ALU.add).then_inc(at["state_done"], 1)
        elif step == "y":
            yq = y[:, q, :]
            dve.wait_ge(at["y_mm"], q + 1)
            dve.wait_ge(at["y_step"], 3 * q + 2)
            nc.vector.tensor_tensor(yq, yq, m.ps[:, 4, 0:D2], ALU.add).then_inc(at["y_read"], 1)
            dve.wait_ge(at["y_read"], q + 1)
            dve.wait_ge(at["skipped"], q + 1)
            nc.vector.tensor_tensor(yq, yq, xtok[:, q, 0:D2], ALU.add).then_inc(at["y_step"], 1)
            dve.wait_ge(at["y_step"], 3 * q + 3)
            nc.vector.tensor_tensor(yq, yq, zdt[:, q, 0:D2], ALU.mult).then_inc(at["y_gated"], 1)


    def tail_scalar(act, at, i, par, step, q=None):
        if step == "rms":
            nc.scalar.activation(ss, ss, ACT.Ln, scale=1.0 / D2, bias=m.eps[:, :]).then_inc(at["rms_log"], 1)
            act.wait_ge(at["rms_log"], 1)
            nc.scalar.activation(ss, ss, ACT.Exp, scale=-0.5).then_inc(at["rms_rstd"], 1)
            act.wait_ge(at["rms_rstd"], 1)
            for q in range(NQ):
                nc.scalar.activation(y[:, q, :], y[:, q, :], ACT.Copy, scale=ss[:, q:q + 1]).then_inc(at["y_normed"], 1)
        elif step == "yt":
            for t in range(N2):
                act.wait_ge(at["yt_mm"], t + 1)
                nc.scalar.copy(yt[:, t, :], m.ps[:, 2 + t, :]).then_inc(at["yt_out"], 1)

    def tail_tensor(pe, at, i, par, step, q=None):
        if step == "yt":
            pe.wait_ge(at["y_normed"], NQ)
            for t in range(N2):
                for q in range(NQ):
                    ins = nc.tensor.transpose(m.ps[:, 2 + t, q * Q:(q + 1) * Q], y[:, q, t * 128:(t + 1) * 128], m.ident[:, :])
                ins.then_inc(at["yt_mm"], 1)
        elif step == "out":
            for c in range(NH):
                for t in range(N2):
                    pe.wait_ge(at["yt_out"], t + 1)
                    ins = nc.tensor.matmul(m.ps[0:P, 5 - c, :], w_out[:, t, c * P:(c + 1) * P], yt[:, t, :],
                                           start=(t == 0), stop=(t == N2 - 1))
                ins.then_inc(at["out_mm"], 1)

    def tail_vector(dve, at, i, par, step, q=None):
        for c in range(NH):
            dve.wait_ge(at["out_mm"], c + 1)
            blk = xs[:, c:c + 1, bass.ds(i * T, T)].rearrange("p a t -> p (a t)")
            nc.vector.tensor_tensor(blk, blk, m.ps[0:P, 5 - c, :], ALU.add).then_inc(at["out_added"], 1)

    def back_gpsimd(pool, at, par):
        def decays(q):
            if q >= 2:
                pool.wait_ge(at["seg_mm"], q - 1)
            nc.gpsimd.tensor_tensor(r[:, q % 2, :].rearrange("p (h i) -> p h i", h=HEADS),
                                    upto.rearrange("p (o i) -> p o i", o=1).broadcast_to([128, HEADS, Q]),
                                    heads(da_of[par][:, q, :], Q), ALU.mult).then_inc(at["r_done"], 1)

        def times_skip(q):
            pool.wait_ge(at["xdt_done"], q + 1)
            nc.gpsimd.tensor_tensor(by_head(xtok[:, q, 0:D2]), by_head(xtok[:, q, 0:D2]), heads(skip), ALU.mult).then_inc(at["skipped"], 1)

        decays(0)
        decays(1)
        times_skip(0)
        times_skip(1)
        decays(2)
        times_skip(2)
        decays(3)
        times_skip(3)

    def thirds(tail_of, back_of, front_of, repeats=False):
        def steps(eng, at, *three):
            def bound(of, do):
                def one(*step):
                    if of is not None:
                        do(eng, at, *of, *step)
                return one

            return [bound(of, do) for of, do in zip((tail_of, back_of, front_of), three)]

        with Stage(nc, *names, repeats=repeats) as sems, nc.Block() as block:
            at = dict(zip(names, sems))

            @block.scalar
            def _(act):
                tail, back, front = steps(act, at, tail_scalar, back_scalar, front_scalar)
                front("take")
                nc.scalar.preload_act_table_set(LN_EXP)
                tail("rms")
                back("tok", 0)
                back("tok", 1)
                tail("yt")
                front("square")
                back("tok", 2)
                back("tok", 3)
                front("rstd")
                back("e", 0)
                front("norm")
                front("zdt", 0)
                front("zdt", 1)
                back("e", 1)
                front("zdt", 2)
                back("e", 2)
                front("zdt", 3)
                front("history")
                front("dt")
                front("xbc", 0)
                back("e", 3)
                front("xbc", 1)
                back("square", 0)
                back("square", 1)
                front("decays")
                front("xbc", 2)
                back("square", 2)
                front("xbc", 3)
                front("xbc", 4)
                back("square", 3)
                front("silu")

            @block.tensor
            def _(pe):
                tail, back, front = steps(pe, at, tail_tensor, back_tensor, front_tensor)
                back("tok", 0)
                back("tok", 1)
                front("mean")
                tail("yt")
                tail("out")
                back("tok", 2)
                back("tok", 3)
                front("var")
                back("seg", 0)
                front("zdt", 0)
                back("y", 0)
                front("zdt", 1)
                back("seg", 1)
                front("zdt", 2)
                back("y", 1)
                back("seg", 2)
                front("zdt", 3)
                back("y", 2)
                front("xbc", 0)
                back("seg", 3)
                front("xbc", 1)
                front("xbc", 2)
                front("sums")
                back("y", 3)
                front("xbc", 3)
                front("xbc", 4)

            @block.vector
            def _(dve):
                tail, back, front = steps(dve, at, tail_vector, back_vector, front_vector)
                back("xdt", 0)
                front("centre")
                back("xdt", 1)
                tail("out")
                back("xdt", 2)
                back("xdt", 3)
                front("scale")
                back("score", 0)
                back("y", 0)
                back("score", 1)
                back("y", 1)
                back("score", 2)
                front("dt_in")
                back("y", 2)
                front("dt")
                back("score", 3)
                front("conv", 1)
                back("y", 3)
                front("conv", 2)
                front("conv", 3)
                front("conv", 4)

            @block.gpsimd
            def _(pool):
                if back_of is not None:
                    back_gpsimd(pool, at, back_of[1])
                if front_of is not None:
                    front_gpsimd(pool, at, front_of[1])

    thirds(None, None, (0, 0))
    thirds(None, (0, 0), (1, 1))
    with nc.Fori(0, NT // 2 - 1) as s:
        thirds((2 * s, 0), (2 * s + 1, 1), (2 * s + 2, 0))
        thirds((2 * s + 1, 1), (2 * s + 2, 0), (2 * s + 3, 1), repeats=True)
    thirds((NT - 2, 0), (NT - 1, 1), None)
    thirds((NT - 1, 1), None, None)


def project(m, xn, xa, w, x, x1):
    nc = m.nc
    with Stage(nc, "proj_mm", "act_taken", "dve_taken", "stored") as (proj_mm, act_taken, dve_taken, stored), nc.Block() as block:
        steps = [(i, c) for i in range(NT) for c in range(N2)]

        @block.sync
        def _(sp):
            for h in range(NH):
                sp.dma_start(x1[:, h, :], x[:, h, :]).then_inc(stored, 16)
            sp.wait_ge(stored, 16 * NH)

        @block.tensor
        def _(pe):
            for n, (i, c) in enumerate(steps):
                if n >= 8:
                    pe.wait_ge(dve_taken if n % 2 else act_taken, n // 2 - 3)
                for t in range(NH):
                    ins = nc.tensor.matmul(m.ps[:, n % 8, :], w[:, t, c * 128:(c + 1) * 128], xn[:, t, i * T:(i + 1) * T],
                                           start=(t == 0), stop=(t == NH - 1))
                ins.then_inc(proj_mm, 1)

        @block.scalar
        def _(act):
            for n, (i, c) in enumerate(steps):
                if n % 2 == 0:
                    act.wait_ge(proj_mm, n + 1)
                    nc.scalar.copy(xa[:, c, i * T:(i + 1) * T], m.ps[:, n % 8, :]).then_inc(act_taken, 1)

        @block.vector
        def _(dve):
            for n, (i, c) in enumerate(steps):
                if n % 2:
                    dve.wait_ge(proj_mm, n + 1)
                    nc.vector.tensor_copy(xa[:, c, i * T:(i + 1) * T], m.ps[:, n % 8, :]).then_inc(dve_taken, 1)


def scan_weights(m, a):
    m.start(0)
    xpw = m.take(K4, N2, P + DTR)
    m.start(SLOTS)
    dtw = m.take(K4, D2)
    aneg = m.take(K4, N2, NS)
    dtb = m.take(K4, N2)
    dsk = m.take(K4, N2)
    BC = 2 * NS
    xw = a["x_proj_w"]
    loads = []
    for k in range(K4):
        src = xw[:, k, :].rearrange("(t p) c -> p t c", p=128)
        for i in range(3):
            loads.append((xpw[:, k, :, BC * i:BC * (i + 1)], src[:, :, DTR:]))
        loads.append((xpw[:, k, :, P:], src[:, :, 0:DTR]))
        loads.append((dtw[P:P + DTR, k, :], a["dt_w"][:, k, :]))
        loads.append((aneg[:, k, :, :], a["A_logs"][k * D2:(k + 1) * D2, :].rearrange("(t p) n -> p t n", p=128)))
        loads.append((dtb[:, k, :], columns(a["dt_b"][k, :], 128)))
        loads.append((dsk[:, k, :], columns(a["Ds"][k * D2:(k + 1) * D2], 128)))
    return (xpw, dtw, aneg, dtb, dsk), loads


def selective_scan(m, xc, y, weights):
    nc = m.nc
    xpw, dtw, aneg, dtb, dsk = weights
    carry = m.take(K4, N2 * NS)
    sp_l = m.take(T)
    sp_w = m.take(T)
    m.start(0)
    m.take(K4, N2, P + DTR)
    bbc = m.take(NS, T)
    delta = m.take(2, N2, T)
    du = m.take(2, N2, T)
    hs = m.take(3, T)
    hc = m.take(2, T)
    dbu = m.take(6, T)
    xd = m.take(T)
    rest = m.take(T)
    mid, low = (m.take(T // 2).bitcast(BF16) for _ in range(2))
    sp_e = m.take(2, T)
    parts = m.take(T).bitcast(BF16).rearrange("p (a b) -> p a b", a=2)
    assert m.top <= 6 * SLOT

    def block_of(k, v, t, i):
        i = (NT - 1 - i) if k >= 2 else i
        if k % 2 == 0:
            return v[:, t:t + 1, bass.ds(i * T, T)].rearrange("p a t -> p (a t)")
        wide = T // H
        return v.rearrange("p t (h w) -> p t w h", w=W)[:, t:t + 1, bass.ds(i * wide, wide), :].rearrange("p a w h -> p (a w) h")

    def shaped(k, v):
        return v if k % 2 == 0 else v.rearrange("p (w h) -> p w h", h=H)

    names = ("xd_mm", "xd_out", "rest_done", "mid_out", "low_done", "parts_out", "dl_mm", "sp_act", "sp_dve", "sp_pool", "bb_mm", "bb_out",
             "da_ready", "db_ready", "scanned", "saved", "c_mm", "hc_ready", "y_mm", "y_added")

    def pe_ahead(pe, at, k, w, i, par, o):
        if w < N2:
            if o and w == 0:
                pe.wait_ge(at["bb_out"], NS * o)
            ins = nc.tensor.matmul(shaped(k, m.ps[0:P + DTR, 7, :]), xpw[:, k, w, :], block_of(k, xc, w, i),
                                   start=(w == 0), stop=(w == N2 - 1))
            if w == N2 - 1:
                ins.then_inc(at["xd_mm"], 1)
        if w in (7, 14, 21):
            t = w // 7 - 1
            pe.wait_ge(at["xd_out"], o + 1)
            if t:
                pe.wait_ge(at["sp_act"], 5 * (N2 * o + t - 1) + 2)
            nc.tensor.matmul(m.ps[:, 7, :], dtw[P:P + DTR, k, t * 128:(t + 1) * 128], xd[P:P + DTR, :],
                             start=True, stop=True, tile_position=(P, 0)).then_inc(at["dl_mm"], 1)
        if 31 <= w < 47:
            n = w - 31
            if n == 0:
                pe.wait_ge(at["parts_out"], 2 * (o + 1))
            if n == 1:
                pe.wait_ge(at["sp_act"], 5 * N2 * (o + 1))
            if NS * o + n >= 2:
                pe.wait_ge(at["bb_out"], NS * o + n - 1)
            nc.tensor.matmul(m.ps[:, 6 + n % 2, :], m.sel[:, n:n + 1].broadcast_to([P, 128]), parts[0:P, par, :],
                             start=True, stop=True).then_inc(at["bb_mm"], 1)

    def act_ahead(act, at, k, w, i, par, o, units=None):
        if w == 5:
            act.wait_ge(at["xd_mm"], o + 1)
            nc.scalar.copy(parts[0:P, par, :], m.ps[0:P, 7, :])
        if w == 6:
            if o:
                act.wait_ge(at["rest_done"], o)
                act.wait_ge(at["dl_mm"], N2 * o)
            nc.scalar.copy(xd[0:P + DTR, :], m.ps[0:P + DTR, 7, :]).then_inc(at["xd_out"], 1)
        if w == 8:
            act.wait_ge(at["rest_done"], o + 1)
            if o:
                act.wait_ge(at["low_done"], o)
            nc.scalar.copy(mid[0:P, :], rest[0:P, :]).then_inc(at["mid_out"], 1)
        if w == 10:
            nc.scalar.copy(parts[32:64, par, :], rest[32:64, :]).then_inc(at["parts_out"], 1)
        if w == 15:
            act.wait_ge(at["low_done"], o + 1)
            nc.scalar.copy(parts[64:96, par, :], low[64:96, :]).then_inc(at["parts_out"], 1)
        if 10 <= w < 34 and (w - 10) % 8 < 5:
            t, j = (w - 10) // 8, (w - 10) % 8
            done = 5 * (N2 * o + t) + j
            bias, e = dtb[:, k, t:t + 1], sp_e[:, (N2 * o + t) % 2, :]
            if j == 0:
                act.wait_ge(at["dl_mm"], N2 * o + t + 1)
                if N2 * o + t >= 2:
                    act.wait_ge(at["sp_pool"], 3 * (N2 * o + t) - 4)
                ins = nc.scalar.activation(e, m.ps[:, 7, :], ACT.Abs, bias=bias)
            elif j == 1:
                ins = nc.scalar.activation(delta[:, par, t, :], m.ps[:, 7, :], ACT.Relu, bias=bias)
            elif j == 2:
                act.wait_ge(at["sp_act"], done - 1)
                ins = nc.scalar.activation(e, e, ACT.Exp, scale=-1.0)
            elif j == 3:
                act.wait_ge(at["sp_act"], done)
                if N2 * o + t:
                    act.wait_ge(at["sp_dve"], N2 * o + t)
                ins = nc.scalar.activation(sp_w, e, ACT.Identity, bias=1.0)
            else:
                act.wait_ge(at["sp_act"], done)
                if N2 * o + t:
                    act.wait_ge(at["sp_pool"], 3 * (N2 * o + t) - 2)
                ins = nc.scalar.activation(sp_l, sp_w, ACT.Ln)
            ins.then_inc(at["sp_act"], 1)
        if 34 <= w < 34 + NS:
            n = w - 34
            act.wait_ge(at["bb_mm"], NS * o + n + 1)
            if units is not None:
                act.wait_ge(at["db_ready"], units + 2 * NS + n + 1)
            nc.scalar.copy(bbc[:, n, :], m.ps[:, 6 + n % 2, :]).then_inc(at["bb_out"], 1)

    def pool_ahead(pool, at, k, w, i, par, o):
        if w == 11:
            pool.wait_ge(at["mid_out"], o + 1)
            if o:
                pool.wait_ge(at["parts_out"], 2 * o)
            nc.gpsimd.tensor_tensor(low[0:P, :], rest[0:P, :], mid[0:P, :], ALU.subtract).then_inc(at["low_done"], 1)
        if 19 <= w < 43 and (w - 19) % 8 in (0, 3, 6):
            t, j = (w - 19) // 8, (w - 19) % 8 // 3
            done = 3 * (N2 * o + t) + j
            e = sp_e[:, (N2 * o + t) % 2, :]
            if j == 0:
                pool.wait_ge(at["sp_dve"], N2 * o + t + 1)
                pool.wait_ge(at["sp_act"], 5 * (N2 * o + t + 1))
                ins = nc.gpsimd.tensor_tensor(e, sp_l, e, ALU.subtract)
            else:
                pool.wait_ge(at["sp_pool"], done)
                if j == 1:
                    ins = nc.gpsimd.tensor_tensor(delta[:, par, t, :], delta[:, par, t, :], e, ALU.add)
                else:
                    ins = nc.gpsimd.tensor_tensor(shaped(k, du[:, par, t, :]), shaped(k, delta[:, par, t, :]),
                                                  block_of(k, xc, t, i), ALU.mult)
            ins.then_inc(at["sp_pool"], 1)

    def dve_ahead(dve, at, w, par, o):
        if w == 6:
            dve.wait_ge(at["xd_out"], o + 1)
            if o:
                dve.wait_ge(at["parts_out"], 2 * o)
                dve.wait_ge(at["low_done"], o)
            nc.vector.tensor_tensor(rest[0:P, :], xd[0:P, :], parts[0:P, par, :], ALU.subtract).then_inc(at["rest_done"], 1)
        if w in (13, 21, 29):
            t = w // 8 - 1
            dve.wait_ge(at["sp_act"], 5 * (N2 * o + t) + 4)
            e = sp_e[:, (N2 * o + t) % 2, :]
            nc.vector.scalar_tensor_tensor(e, sp_w, 1.0, e, ALU.subtract, ALU.subtract).then_inc(at["sp_dve"], 1)

    with Stage(nc, "exped", "ds_summed", *names) as (exped, ds_summed, *sems), nc.Block() as block:
        at = dict(zip(names, sems))

        @block.vector
        def _(dve):
            nc.vector.memset(carry, 0.0)
            for k in range(1, K4):
                nc.vector.tensor_tensor(dsk[:, 0, :], dsk[:, 0, :], dsk[:, k, :], ALU.add).then_inc(ds_summed, 1)
                dve.wait_ge(ds_summed, k)
            for w in range(TAIL):
                dve_ahead(dve, at, w, 0, 0)
                if w % 8 == 0 and w // 8 < N2:
                    nc.vector.tensor_scalar(y[:, w // 8, :], xc[:, w // 8, :], dsk[:, 0, w // 8:w // 8 + 1], None, ALU.mult)

        @block.tensor
        def _(pe):
            for w in range(TAIL):
                pe_ahead(pe, at, 0, w, 0, 0, 0)

        @block.scalar
        def _(act):
            nc.scalar.preload_act_table_set(LN_EXP)
            nc.scalar.activation(aneg, aneg, ACT.Exp).then_inc(exped, 1)
            for w in range(TAIL):
                act_ahead(act, at, 0, w, 0, 0, 0)
            act.wait_ge(exped, 1)
            nc.scalar.mul(aneg, aneg, -1.0)

        @block.gpsimd
        def _(pool):
            for w in range(TAIL):
                pool_ahead(pool, at, 0, w, 0, 0, 0)

    BLOCKS = 2 * K4
    ALL = BLOCKS * UNITS

    def unit(v):
        return v // UNITS, v % UNITS // NS, v % NS

    with nc.Fori(0, NT // 2) as pair:
        def ahead(b):
            return (b // 2, 2 * pair + b % 2) if b < BLOCKS else (0, (2 * pair + 2) % NT)

        with Stage(nc, *names, repeats=True) as sems, nc.Block() as block:
            at = dict(zip(names, sems))

            @block.tensor
            def _(pe):
                def add_up(v):
                    g = v // NS
                    if v % NS == 0 and g >= 2:
                        pe.wait_ge(at["y_added"], g - 1)
                    nc.tensor.matmul(m.ps[:, g % 2, :], m.ident[:, :], hc[:, v % 2, :],
                                     start=(v % NS == 0), stop=(v % NS == NS - 1)).then_inc(at["y_mm"], 1)

                def spread_c(v):
                    b, t, n = unit(v)
                    if b and v % UNITS == 0:
                        pe.wait_ge(at["parts_out"], 2 * b)
                    nc.tensor.matmul(m.ps[:, 4 + v % 2, :], m.sel[:, NS + n:NS + n + 1].broadcast_to([P, 128]),
                                     parts[0:P, b % 2, :], start=True, stop=True).then_inc(at["c_mm"], 1)

                spread_c(0)
                spread_c(1)
                for v in range(ALL):
                    b, t, n = unit(v)
                    k, i = ahead(b + 1)
                    pe_ahead(pe, at, k, v % UNITS, i, (b + 1) % 2, b)
                    pe.wait_ge(at["hc_ready"], v + 1)
                    if v + 2 < ALL:
                        spread_c(v + 2)
                    add_up(v)

            @block.scalar
            def _(act):
                nc.scalar.preload_act_table_set(LN_EXP)

                def save(v):
                    b, t, n = unit(v)
                    k = b // 2
                    last = 0 if k >= 2 else T - 1
                    act.wait_ge(at["scanned"], v + 1)
                    nc.scalar.copy(carry[:, k, t * NS + n:t * NS + n + 1], hs[:, v % 3, last:last + 1]).then_inc(at["saved"], 1)

                for v in range(ALL):
                    b, t, n = unit(v)
                    if v >= 2:
                        act.wait_ge(at["scanned"], v - 1)
                    if b and n == 0:
                        act.wait_ge(at["sp_pool"], 3 * (N2 * (b - 1) + t + 1))
                    nc.scalar.activation(m.ps[:, 2 + v % 2, :], delta[:, b % 2, t, :], ACT.Exp,
                                         scale=aneg[:, b // 2, t, n:n + 1]).then_inc(at["da_ready"], 1)
                    if v >= 2:
                        save(v - 2)
                    w = v % UNITS
                    if b and w + UNITS < TAIL:
                        k, i = ahead(b)
                        act_ahead(act, at, k, w + UNITS, i, b % 2, b - 1, (b - 1) * UNITS)
                    k, i = ahead(b + 1)
                    act_ahead(act, at, k, w, i, (b + 1) % 2, b, b * UNITS)
                save(ALL - 2)
                save(ALL - 1)
                for w in range(UNITS, TAIL):
                    act_ahead(act, at, 0, w, None, 0, BLOCKS - 1, (BLOCKS - 1) * UNITS)

            @block.gpsimd
            def _(pool):
                for v in range(0, ALL, 2):
                    b, t, n = unit(v)
                    if v >= 6:
                        pool.wait_ge(at["scanned"], v - 4)
                    if b and t == 0:
                        pool.wait_ge(at["bb_out"], NS * (b - 1) + n + 2)
                        if n == 0:
                            pool.wait_ge(at["sp_pool"], 3 * N2 * b)
                    both = du[:, b % 2, t, :].rearrange("p (o l) -> p o l", o=1).broadcast_to([128, 2, T])
                    nc.gpsimd.tensor_tensor(dbu[:, v % 6:v % 6 + 2, :], both, bbc[:, n:n + 2, :], ALU.mult).then_inc(at["db_ready"], 2)
                    k, i = ahead(b + 1)
                    for w in (v % UNITS, v % UNITS + 1):
                        pool_ahead(pool, at, k, w, i, (b + 1) % 2, b)

            @block.vector
            def _(dve):
                def times_c(v):
                    dve.wait_ge(at["scanned"], v + 1)
                    dve.wait_ge(at["c_mm"], v + 1)
                    if v >= 2:
                        dve.wait_ge(at["y_mm"], v - 1)
                    nc.vector.tensor_tensor(hc[:, v % 2, :], hs[:, v % 3, :], m.ps[:, 4 + v % 2, :],
                                            ALU.mult).then_inc(at["hc_ready"], 1)

                def take_y(g):
                    b, t, n = unit(g * NS)
                    k = b // 2
                    dve.wait_ge(at["y_mm"], NS * (g + 1))
                    if k:
                        dve.wait_ge(at["y_added"], 2 * N2 * k)
                    out = block_of(k, y, t, 2 * pair + b % 2)
                    nc.vector.tensor_tensor(out, out, shaped(k, m.ps[:, g % 2, :]), ALU.add).then_inc(at["y_added"], 1)

                for v in range(ALL):
                    b, t, n = unit(v)
                    k = b // 2
                    flip = (lambda x: x[:, ::-1]) if k >= 2 else (lambda x: x)
                    dve.wait_ge(at["da_ready"], v + 1)
                    dve.wait_ge(at["db_ready"], v + 1)
                    if v >= 3:
                        dve.wait_ge(at["saved"], v - 2)
                        dve.wait_ge(at["hc_ready"], v - 2)
                    if b % 2:
                        dve.wait_ge(at["saved"], v - UNITS + 1)
                    nc.vector.tensor_tensor_scan(flip(hs[:, v % 3, :]), flip(m.ps[:, 2 + v % 2, :]), flip(dbu[:, v % 6, :]),
                                                 carry[:, k, t * NS + n:t * NS + n + 1], ALU.mult, ALU.add).then_inc(at["scanned"], 1)
                    if v:
                        times_c(v - 1)
                    dve_ahead(dve, at, v % UNITS, (b + 1) % 2, b)
                    if v >= NS and n == 3:
                        take_y(v // NS - 1)
                times_c(ALL - 1)
                take_y(ALL // NS - 1)


def finish_scan(m, y, x, x1, a):
    nc = m.nc
    m.start(2)
    wz = m.take(NH, D2, parts=P)
    wo = m.take(N2, C)
    cols = m.take(2, N2)
    lns = [LayerNorm(m, N2, 128, cols[:, 0, :], cols[:, 1, :], "ab"[i]) for i in range(2)]
    xn = [m.take(NH, T, parts=P) for _ in range(2)]
    assert m.top <= 6 * SLOT
    m.start(9)
    yin = [m.take(N2, T) for _ in range(2)]
    sz = [m.take(N2, T) for _ in range(2)]
    h = [m.take(N2, T) for _ in range(2)]
    names = ["filled", "brought", "x_in_a", "x_in_b", "taken", "z_mm", "z_out", "gated", "out_mm",
             "summed"] + lns[0].names + lns[1].names

    def step(back, front, repeats=False):
        def tokens(v, pair, i):
            return v[:, :, bass.ds((2 * pair + i) * T, T)]

        with Stage(nc, *names, repeats=repeats) as sems, nc.Block() as block:
            at = dict(zip(names, sems))

            @block.sync
            def _(sp):
                if front is not None:
                    for i in range(2):
                        sp.dma_start(tokens(x, front, i), tokens(x1, front, i)).then_inc(at["x_in_" + "ab"[i]], 16)
                if back is None:
                    bring(m, sp, at["brought"], [
                        (wz, a["in_proj_w"].rearrange("(t p) o -> p t o", p=P)[:, :, D2:]),
                        (wo, a["out_proj_w"].rearrange("(t p) o -> p t o", p=128)),
                        (cols[:, 0, :], columns(a["out_norm_w"], 128)), (cols[:, 1, :], columns(a["out_norm_b"], 128))])

            @block.scalar
            def _(act):
                if back is not None:
                    for i in range(2):
                        for t in range(N2):
                            nc.scalar.activation(h[i][:, t, :], lns[i].xc[:, t, :], ACT.Identity, scale=lns[i].wcol[:, t:t + 1],
                                                 bias=lns[i].bcol[:, t:t + 1]).then_inc(at[lns[i].key("ln_out")], 1)
                    for u in range(2 * N2):
                        act.wait_ge(at["z_mm"], u + 1)
                        nc.scalar.activation(sz[u // N2][:, u % N2, :], m.ps[:, 4 + u % 2, :], ACT.Silu).then_inc(at["z_out"], 1)
                if front is not None:
                    nc.scalar.preload_act_table_set(LN_EXP)
                    for i in range(2):
                        nc.scalar.copy(yin[i], tokens(y, front, i)).then_inc(at["taken"], 1)
                    for i in range(2):
                        lns[i].act_square(act, at)
                    for i in range(2):
                        lns[i].act_rstd(act, at, 2 * i + 1)

            @block.tensor
            def _(pe):
                def out_proj(i):
                    for c in range(NH):
                        if i:
                            pe.wait_ge(at["summed"], c + 1)
                        for t in range(N2):
                            pe.wait_ge(at["gated"], i * N2 + t + 1)
                            ins = nc.tensor.matmul(m.ps[0:P, 6 + c, :], wo[:, t, c * P:(c + 1) * P], h[i][:, t, :],
                                                   start=(t == 0), stop=(t == N2 - 1))
                        ins.then_inc(at["out_mm"], 1)

                if back is not None:
                    for u in range(2 * N2):
                        i, o = u // N2, u % N2
                        if u >= 2:
                            pe.wait_ge(at["z_out"], u - 1)
                        for t in range(NH):
                            ins = nc.tensor.matmul(m.ps[:, 4 + u % 2, :], wz[:, t, o * 128:(o + 1) * 128], xn[i][:, t, :],
                                                   start=(t == 0), stop=(t == NH - 1))
                        ins.then_inc(at["z_mm"], 1)
                    out_proj(0)
                if front is not None:
                    if back is None:
                        pe.wait_ge(at["filled"], 2)
                    for i in range(2):
                        pe.wait_ge(at["taken"], i + 1)
                        lns[i].pe_mean(pe, at, yin[i], 2 * i)
                if back is not None:
                    out_proj(1)
                if front is not None:
                    for i in range(2):
                        lns[i].pe_var(pe, at, 2 * i + 1)

            @block.vector
            def _(dve):
                def gate(i):
                    for t in range(N2):
                        dve.wait_ge(at[lns[i].key("ln_out")], t + 1)
                        dve.wait_ge(at["z_out"], i * N2 + t + 1)
                        nc.vector.tensor_tensor(h[i][:, t, :], h[i][:, t, :], sz[i][:, t, :], ALU.mult).then_inc(at["gated"], 1)

                def add_up(i):
                    for c in range(NH):
                        dve.wait_ge(at["out_mm"], i * NH + c + 1)
                        blk = tokens(x, back, i)[:, c, :]
                        nc.vector.tensor_tensor(blk, blk, m.ps[0:P, 6 + c, :], ALU.add).then_inc(at["summed"], 1)
                        dve.wait_ge(at["summed"], i * NH + c + 1)
                        block_stats(m, blk, c, 2 * back + i)

                if back is None:
                    for one in lns:
                        one.constants().then_inc(at["filled"], 1)
                if back is not None:
                    gate(0)
                    gate(1)
                if front is not None:
                    if back is not None:
                        dve.wait_ge(at["z_mm"], 2 * N2)
                    for i in range(2):
                        dve.wait_ge(at["x_in_" + "ab"[i]], 16)
                        for t in range(NH):
                            nc.vector.tensor_scalar(xn[i][:, t, :], tokens(x, front, i)[:, t, :], m.gn_mean[:, t:t + 1],
                                                    m.gn_rstd[:, t:t + 1], ALU.subtract, ALU.mult)
                if back is not None:
                    add_up(0)
                if front is not None:
                    for i in range(2):
                        if back is not None:
                            dve.wait_ge(at[lns[i].key("ln_out")], N2)
                        lns[i].dve_centre(dve, at, yin[i], 2 * i)
                if back is not None:
                    add_up(1)
                if front is not None:
                    for i in range(2):
                        lns[i].dve_scale(dve, at)

    step(None, 0)
    with nc.Fori(0, NT // 2 - 1) as s:
        step(s, s + 1, repeats=True)
    step(NT // 2 - 1, None)


def layers(nc, x, out, x1, l0, l1, l2, l3, samples=B):
    with ExitStack() as ctx:
        m = Chip(nc, ctx)
        Stage.held = None
        constants(m)
        x1v = x1.rearrange("(t p) l -> p t l", p=P)
        with nc.Fori(0, samples) as b:
            xb = x[bass.ds(b, 1)].rearrange("a (t p) l -> p (a t) l", p=P)
            ob = out[bass.ds(b, 1)].rearrange("a (t p) l -> p (a t) l", p=P)
            s01, s23, s45 = m.slots(0, NH, P), m.slots(2, NH, P), m.slots(4, NH, P)

            taps = Taps(m, NH, P, l0["cpe1_w"], l0["cpe1_b"], own=True)
            group_norm(m, s01, s23, taps, load=xb)
            taps_2 = Taps(m, NH, P, l0["cpe2_w"], l0["cpe2_b"], own=True)
            weights, loads = ssd_weights(m, l0)
            conv3x3(m, s23, s45, taps, loads=loads)
            ssd(m, s45, weights, taps_2)
            weights, loads = mlp_weights(m, l0)
            conv3x3(m, s45, s23, taps_2, loads=loads)
            mlp(m, s23, s01, weights)
            taps = Taps(m, N2, 128, l1["conv_w"], l1["conv_b"], slot=8)
            m.start(7)
            w_in = m.take(NH, D2, parts=P)
            group_norm(m, s01, s23, taps, loads=[(w_in, l1["in_proj_w"].rearrange("(t p) o -> p t o", p=P)[:, :, 0:D2])],
                       have_stats=True)
            xa, xc, y = m.slots(4, N2), m.slots(9, N2), m.slots(6, N2)
            project(m, s23, xa, w_in, s01, x1v)
            weights, loads = scan_weights(m, l1)
            conv3x3(m, xa, xc, taps, silu=True, loads=loads)
            selective_scan(m, xc, y, weights)
            finish_scan(m, y, s01, x1v, l1)
            taps = Taps(m, NH, P, l2["w"], l2["b"])
            group_norm(m, s01, s23, taps, have_stats=True)
            conv3x3(m, s23, s45, taps, residual=s01)
            taps = Taps(m, NH, P, l3["w"], l3["b"])
            group_norm(m, s45, s23, taps)
            conv3x3(m, s23, s01, taps, residual=s45, out=ob)
            nc.all_engine_barrier()


LAYER_INS = {
    "L0_conv_": ("cpe1_w", "cpe1_b", "ln1_w", "ln1_b", "in_proj_w", "conv1d_w", "conv1d_b", "dt_bias", "A_log", "D_skip",
                 "rms_w", "out_proj_w", "cpe2_w", "cpe2_b", "ln2_w", "ln2_b", "fc1_w", "fc1_b", "fc2_w", "fc2_b"),
    "L1_conv_": ("in_proj_w", "conv_w", "conv_b", "x_proj_w", "dt_w", "dt_b", "A_logs", "Ds", "out_norm_w", "out_norm_b",
                 "out_proj_w"),
    "L2_conv_": ("w", "b"),
    "L3_conv_": ("w", "b"),
}
RENAMED = {"x_proj_w": "x_proj_weight", "dt_w": "dt_projs_weight", "dt_b": "dt_projs_bias"}


def laid_out(name, v):
    import numpy as np
    v = np.asarray(v)
    if name == "x":
        v = v.transpose(0, 3, 1, 2).reshape(v.shape[0], C, L)
    elif name in ("in_proj_w", "out_proj_w", "fc1_w", "fc2_w"):
        v = v.T
    elif name in ("cpe1_w", "cpe2_w", "conv_w"):
        v = v.reshape(-1, 9)
    elif name == "w":
        v = v.reshape(9, C).T
    elif name in ("x_proj_w", "dt_w"):
        v = v.transpose(2, 0, 1)
    return np.ascontiguousarray(v)


def program(nc, arrays, samples=B):
    def dram(name, v):
        return nc.dram_tensor(name, v.shape, mybir.dt.from_np(v.dtype), kind="ExternalInput").ap()

    x = dram("x", arrays["x"])
    params = [{n: dram(prefix + n, arrays[prefix + n]) for n in names} for prefix, names in LAYER_INS.items()]
    out = nc.dram_tensor("out", (samples, C, L), F32, kind="ExternalOutput").ap()
    x1 = nc.dram_tensor("x1", (C, L), F32, kind="Internal").ap()
    layers(nc, x, out, x1, *params, samples=samples)


def kernel(**inputs):
    import concourse.bacc as bacc
    from concourse.bass_utils import run_bass_kernel_spmd

    nc = bacc.Bacc("TRN2", target_bir_lowering=False, num_devices=1)
    arrays = {"x": laid_out("x", inputs["x"])}
    for prefix, names in LAYER_INS.items():
        for n in names:
            arrays[prefix + n] = laid_out(n, inputs[prefix + RENAMED.get(n, n)])
    program(nc, arrays)
    r = run_bass_kernel_spmd(nc, [arrays], core_ids=[0])
    return r.results[0]["out"].reshape(B, C, H, W).transpose(0, 2, 3, 1)
```
